# Optimizing a Trainium2 kernel written in Bass

```python
import numpy as np
import jax
import jax.numpy as jnp

def _softmax(x, axis=-1):
    return jax.nn.softmax(x, axis=axis)

def _gelu(x):
    return jax.nn.gelu(x, approximate=True)

def _silu(x):
    return jax.nn.silu(x)

def _sigmoid(x):
    return jax.nn.sigmoid(x)

def _layernorm(x, axis=-1, eps=1e-05):
    m = jnp.mean(x, axis=axis, keepdims=True)
    v = jnp.var(x, axis=axis, keepdims=True)
    return (x - m) / jnp.sqrt(v + eps)

def _scatter_add(tgt, idx, src, axis=0):
    return tgt.at[idx].add(src)

def _segment_sum(src, seg, n):
    return jax.ops.segment_sum(src, seg, n)
kernel_name = 'mk_adj_preln_d4_adj_r2_3ce88e'

def setup_inputs(seed: int=0):
    np.random.seed(seed)
    _w = jnp.asarray

    def _rec_inputs():
        import jax
        import jax.numpy as jnp
        _gk = jax.random.key(seed)
        x = -0.0002928 + 1 * jax.random.normal(jax.random.fold_in(_gk, 1), (32, 256, 128), jnp.float32)
        _a = jax.random.bernoulli(jax.random.fold_in(_gk, 2), 0.015625, (256, 256))
        _a = jnp.logical_or(_a, jnp.swapaxes(_a, -1, -2))
        _a = jnp.logical_or(_a, jnp.eye(256, dtype=bool))
        _af = _a.astype(jnp.float32)
        adj = _af
        return (x, adj)
    x, adj = _rec_inputs()

    def _L0_gnn_setup():
        import jax, jax.numpy as jnp
        import numpy as np
        B, N, D = (4, 4096, 128)
        key = jax.random.key(seed)
        kx, ka, kq, kk, kv = jax.random.split(key, 5)
        x = jax.random.normal(kx, (B, N, D), dtype=jnp.float32)
        mask = (jax.random.uniform(ka, (N, N)) < 0.05).astype(jnp.float32)
        A_shape = jnp.clip(mask + jnp.eye(N, dtype=jnp.float32), 0.0, 1.0)
        q = jax.random.normal(kq, (D, D), dtype=jnp.float32)
        k = jax.random.normal(kk, (D, D), dtype=jnp.float32)
        v = jax.random.normal(kv, (D, D), dtype=jnp.float32)
        return {'x': x, 'A_shape': A_shape, 'q': q, 'k': k, 'v': v}
    _L0_gnn_all = _L0_gnn_setup()
    _L0_gnn_in = {k: v for k, v in _L0_gnn_all.items() if k in ('q', 'k', 'v')}
    del _L0_gnn_all

    def _L1_gnn_setup():
        import jax, jax.numpy as jnp
        import numpy as np
        from jax import lax
        CONV_ORDER = 3

        def _chebyshev(adj, x, order):

            def step(carry, _):
                nxt = jnp.einsum('ij,bjc->bic', adj, carry)
                return (nxt, nxt)
            _, xs = lax.scan(step, x, None, length=order)
            return jnp.moveaxis(xs, 0, -1)
        key = jax.random.key(seed)
        k1, k2, k3, k4 = jax.random.split(key, 4)
        B, E, C_in, C_out, K, n_adjs = (8, 2048, 128, 128, CONV_ORDER, 2)
        x_1 = jax.random.normal(k1, (B, E, C_in), dtype=jnp.float32)
        adj0 = jax.random.normal(k2, (E, E), dtype=jnp.float32) / np.sqrt(E)
        adj1 = jax.random.normal(k3, (E, E), dtype=jnp.float32) / np.sqrt(E)
        kdim = K * n_adjs + 1
        std = 1.414 * np.sqrt(2.0 / float((C_in + C_out) * kdim))
        weight_1 = std * jax.random.normal(k4, (C_in, C_out, kdim), dtype=jnp.float32)
        return {'x_1': x_1, 'adj0': adj0, 'adj1': adj1, 'weight_1': weight_1}
    _L1_gnn_all = _L1_gnn_setup()
    _L1_gnn_in = {k: v for k, v in _L1_gnn_all.items() if k in ('weight_1',)}
    del _L1_gnn_all

    def _L2_gnn_setup():
        import jax, jax.numpy as jnp
        import numpy as np
        B, N, F_IN, F_OUT = (8, 1024, 128, 128)
        ALPHA = 0.1
        NEG_BIG = -9000000000000000.0

        def _pair_indices(n):
            m = jnp.arange(n)[:, None] * n + jnp.arange(n)[None, :]
            nn = n * n
            k1, k2 = (2 * m, 2 * m + 1)
            idx1 = jnp.where(k1 < nn, k1 // n, k1 % n)
            idx2 = jnp.where(k2 < nn, k2 // n, k2 % n)
            return (idx1, idx2)
        key = jax.random.key(seed)
        k1, k2, k3, k4 = jax.random.split(key, 4)
        x = jax.random.normal(k1, (B, N, F_IN), dtype=jnp.float32)
        adj = jnp.ones((N, N), dtype=jnp.float32) - jnp.eye(N, dtype=jnp.float32)
        others_weight = jax.random.normal(k2, (F_IN, F_OUT), dtype=jnp.float32) * (1.0 / np.sqrt(F_OUT))
        self_weight = jax.random.normal(k3, (F_IN, F_OUT), dtype=jnp.float32) * (1.0 / np.sqrt(F_OUT))
        att_weight = jax.random.normal(k4, (2 * F_OUT, 1), dtype=jnp.float32)
        return {'x': x, 'adj': adj, 'others_weight': others_weight, 'self_weight': self_weight, 'att_weight': att_weight}
    _L2_gnn_all = _L2_gnn_setup()
    _L2_gnn_in = {k: v for k, v in _L2_gnn_all.items() if k in ('others_weight', 'self_weight', 'att_weight')}
    del _L2_gnn_all

    def _L3_gnn_setup():
        import jax, jax.numpy as jnp
        import numpy as np
        NEG = -9000000000000000.0
        key = jax.random.key(seed)
        k1, k2, k3, k4 = jax.random.split(key, 4)
        B, N, F_in, F_out, MAX_E = (8192, 16, 128, 128, 128)
        inp = jax.random.normal(k1, (B, N, F_in), dtype=jnp.float32)
        adj = jax.random.uniform(k2, (N, N), dtype=jnp.float32)
        limit = 1.414 * np.sqrt(6.0 / (F_in + F_out))
        W = jax.random.uniform(k3, (2, F_in, F_out), dtype=jnp.float32, minval=-limit, maxval=limit)
        e = jnp.ones((1, MAX_E), dtype=jnp.float32)
        stdv = 1.0 / np.sqrt(F_out)
        bias = jax.random.uniform(k4, (F_out,), dtype=jnp.float32, minval=-stdv, maxval=stdv)
        return {'input': inp, 'adj': adj, 'W': W, 'e': e, 'bias': bias}
    _L3_gnn_all = _L3_gnn_setup()
    _L3_gnn_in = {k: v for k, v in _L3_gnn_all.items() if k in ('W', 'e', 'bias')}
    del _L3_gnn_all
    return {'x': x, 'adj': adj, 'L0_gnn_q': _L0_gnn_in['q'], 'L0_gnn_k': _L0_gnn_in['k'], 'L0_gnn_v': _L0_gnn_in['v'], 'L1_gnn_weight_1': _L1_gnn_in['weight_1'], 'L2_gnn_others_weight': _L2_gnn_in['others_weight'], 'L2_gnn_self_weight': _L2_gnn_in['self_weight'], 'L2_gnn_att_weight': _L2_gnn_in['att_weight'], 'L3_gnn_W': _L3_gnn_in['W'], 'L3_gnn_e': _L3_gnn_in['e'], 'L3_gnn_bias': _L3_gnn_in['bias']}

def reference(x, adj, L0_gnn_q, L0_gnn_k, L0_gnn_v, L1_gnn_weight_1, L2_gnn_others_weight, L2_gnn_self_weight, L2_gnn_att_weight, L3_gnn_W, L3_gnn_e, L3_gnn_bias):
    import jax
    import jax.numpy as jnp

    def _L0_gnn_ref(x, A_shape, q, k, v):
        import jax, jax.numpy as jnp
        import numpy as np
        B, N, D = (4, 4096, 128)
        input_dimension = x.shape[-1]
        Q = x @ q
        K = x @ k
        A = jnp.einsum('bnd,bmd->bnm', Q, K)
        A = A / jnp.sqrt(jnp.float32(input_dimension))
        A = jnp.tanh(A / 8.0) * 8.0
        A = jnp.exp(A) * A_shape
        A = A / jnp.sum(A, axis=-1, keepdims=True)
        out = A @ x @ v
        return out

    def _L1_gnn_ref(x_1, adj0, adj1, weight_1):
        import jax, jax.numpy as jnp
        import numpy as np
        from jax import lax
        CONV_ORDER = 3

        def _chebyshev(adj, x, order):

            def step(carry, _):
                nxt = jnp.einsum('ij,bjc->bic', adj, carry)
                return (nxt, nxt)
            _, xs = lax.scan(step, x, None, length=order)
            return jnp.moveaxis(xs, 0, -1)
        parts = [x_1[..., None], _chebyshev(adj0, x_1, CONV_ORDER), _chebyshev(adj1, x_1, CONV_ORDER)]
        x_all = jnp.concatenate(parts, axis=3)
        y_1 = jnp.einsum('bnik,iok->bno', x_all, weight_1)
        return y_1

    def _L2_gnn_ref(x, adj, others_weight, self_weight, att_weight):
        import jax, jax.numpy as jnp
        import numpy as np
        B, N, F_IN, F_OUT = (8, 1024, 128, 128)
        ALPHA = 0.1
        NEG_BIG = -9000000000000000.0

        def _pair_indices(n):
            m = jnp.arange(n)[:, None] * n + jnp.arange(n)[None, :]
            nn = n * n
            k1, k2 = (2 * m, 2 * m + 1)
            idx1 = jnp.where(k1 < nn, k1 // n, k1 % n)
            idx2 = jnp.where(k2 < nn, k2 // n, k2 % n)
            return (idx1, idx2)
        b, n, _ = x.shape
        f_out = others_weight.shape[1]
        h = x @ others_weight
        a1 = att_weight[:f_out, 0]
        a2 = att_weight[f_out:, 0]
        u1 = h @ a1
        u2 = h @ a2
        idx1, idx2 = _pair_indices(n)
        e = u1[:, idx1] + u2[:, idx2]
        e = jnp.where(e >= 0, e, ALPHA * e)
        att = jnp.where(adj > 0, e, NEG_BIG)
        att = jax.nn.softmax(att, axis=1)
        out = jnp.einsum('bik,bkl->bil', att, h)
        out = out + x @ self_weight
        return out

    def _L3_gnn_ref(input, adj, W, e, bias):
        import jax, jax.numpy as jnp
        import numpy as np
        NEG = -9000000000000000.0
        h0 = jnp.einsum('bnf,fg->bng', input, W[0])
        h1 = jnp.einsum('bnf,fg->bng', input, W[1])
        m = adj > 0
        idx = jnp.cumsum(m.reshape(-1).astype(jnp.int32)) - 1
        vals = e[0][idx].reshape(adj.shape)
        A = jnp.where(m, vals, jnp.float32(NEG))
        A = jax.nn.softmax(A, axis=1)
        M = jnp.eye(adj.shape[0], dtype=A.dtype)
        out = jnp.einsum('ij,bjg->big', A * M, h0) + jnp.einsum('ij,bjg->big', A * (1.0 - M), h1)
        return out + bias[None, None, :]
    h = jnp.maximum(_layernorm(x, axis=-1), 0.0)
    x = x + _L0_gnn_ref(h, adj, L0_gnn_q, L0_gnn_k, L0_gnn_v)
    h = jnp.maximum(_layernorm(x, axis=-1), 0.0)
    x = x + _L1_gnn_ref(h, adj, adj, L1_gnn_weight_1)
    h = jnp.maximum(_layernorm(x, axis=-1), 0.0)
    x = x + _L2_gnn_ref(h, adj, L2_gnn_others_weight, L2_gnn_self_weight, L2_gnn_att_weight)
    h = jnp.maximum(_layernorm(x, axis=-1), 0.0)
    x = x + _L3_gnn_ref(h, adj, L3_gnn_W, L3_gnn_e, L3_gnn_bias)
    return x

_drawn_inputs = setup_inputs


def setup_inputs(seed=0):
    import zlib

    import numpy as np

    out = dict(_drawn_inputs(seed))
    spreads = {'L3_gnn_e': (1.0, 0.6)}
    factors = {'L2_gnn_others_weight': 23.013,
     'L2_gnn_self_weight': 35.666,
     'L2_gnn_att_weight': 37.759,
     'L3_gnn_W': 29.065,
     'L3_gnn_bias': 200.0}
    for name, (base, spread) in spreads.items():
        noise = np.random.default_rng([zlib.crc32(name.encode()), seed]).standard_normal(out[name].shape)
        drawn = base * np.exp(spread * noise) if base else spread * noise
        out[name] = jnp.asarray(drawn.astype(out[name].dtype))
    for name, factor in factors.items():
        out[name] = (out[name] * factor).astype(out[name].dtype)
    return out
```

```python
import math
from contextlib import ExitStack

import concourse.bass as bass
from concourse import mybir


def four_layer_gnn(nc, x, adj, q, k, v, w_cheb, w_others, w_self, w_att, w_pair, e_vals, bias, out):
    fp32 = mybir.dt.float32
    ALU = mybir.AluOpType
    ACT = mybir.ActivationFunctionType
    AX = mybir.AxisListType

    P = 128
    B, N, D = x.shape
    assert D == P and N == 2 * P
    T = N // P
    GB = 2
    NG = B // GB
    TG = T * GB
    CH = TG * D
    LAYERS = 4
    SCORE_SCALE = 1.0 / (8.0 * math.sqrt(D))
    EPS = 1e-5
    SLOPE = 0.1
    NEG = -9.0e15
    NEG_PRE = NEG / SLOPE
    HUGE = 3.0e38
    KW = w_cheb.shape[2]
    HOPS = (KW - 1) // 2
    NE = e_vals.shape[1]
    assert NE == P and NG > LAYERS

    ctx = ExitStack()
    with ctx:
        def sb(name, shape, dt=fp32):
            return ctx.enter_context(nc.sbuf_tensor(name, shape, dt))

        def sem(name):
            return ctx.enter_context(nc.semaphore(name))

        def per_layer(name, layers=range(LAYERS)):
            return {n: sem(f"{name}{n}") for n in layers}

        x_all = sb("x_all", [P, NG, TG, D])
        xn = [sb(f"xn{n}", [P, TG, D]) for n in range(LAYERS)]
        hT = [sb(f"hT{n}", [P, TG, P]) for n in range(LAYERS)]
        stats = [sb(f"stats{n}", [P, TG, 6]) for n in range(LAYERS)]
        meanvar = [sb(f"meanvar{n}", [P, TG, 2]) for n in range(LAYERS)]
        var_eps = [sb(f"var_eps{n}", [P, TG]) for n in range(LAYERS)]
        rstd = [sb(f"rstd{n}", [P, TG]) for n in range(LAYERS)]
        minus_half, eps_t = sb("minus_half", [P, TG]), sb("eps_t", [P, TG])

        ident = sb("ident", [P, P])
        adj_nat = sb("adj_nat", [P, T, N])
        adjT = sb("adjT", [P, T, N])

        q_nat, k_nat, v_sb = sb("q_nat", [P, D]), sb("k_nat", [P, D]), sb("v_sb", [P, D])
        qkT = sb("qkT", [P, 2, D])
        m_qk = sb("m_qk", [P, D])
        gT = sb("gT", [P, TG, P])
        hv1 = sb("hv1", [P, TG, D + 1])
        tanh_s = sb("tanh_s", [P, GB, T, N])
        exp_s = sb("exp_s", [P, GB, T, N])
        pT = sb("pT", [P, GB, T, N])
        row_inv = sb("row_inv", [P, GB, T])

        w_raw = sb("w_raw", [P, D, KW])
        w_hop = sb("w_hop", [P, HOPS + 1, D])
        z = [sb(f"z{n}", [P, TG, D]) for n in range(HOPS)]

        others = sb("others", [P, D])
        w_selfs = sb("w_selfs", [P, D])
        att_cols = sb("att_cols", [P, 2])
        othersT = sb("othersT", [P, D])
        u_cols = sb("u_cols", [P, 2])
        u_sum = sb("u_sum", [P, P])
        up_bound = sb("up_bound", [P, T, P])
        low_mask = sb("low_mask", [P, T, P])
        any_up, any_low, edgeless = sb("any_up", [P, T]), sb("any_low", [P, T]), sb("edgeless", [P, T])
        low_count, low_bound = sb("low_count", [P, T]), sb("low_bound", [P, T])
        e_min = sb("e_min", [P, TG, P])
        e_lr = sb("e_lr", [P, TG, P])
        p2 = sb("p2", [P, TG, P])
        t_min, t_lr = sb("t_min", [P, TG]), sb("t_lr", [P, TG])
        e_max, j_max, neg_max = sb("e_max", [P, TG]), sb("j_max", [P, TG]), sb("neg_max", [P, TG])
        t_diff, w_low, low_sum = sb("t_diff", [P, TG]), sb("w_low", [P, TG]), sb("low_sum", [P, TG])
        up_sum, all_sum, col_inv = sb("up_sum", [P, TG]), sb("all_sum", [P, TG]), sb("col_inv", [P, TG])
        hh_up, hh_low = sb("hh_up", [P, TG, D]), sb("hh_low", [P, TG, D])

        w01 = sb("w01", [P, 2, D])
        e_col, e_cut, e_last = sb("e_col", [P, 1]), sb("e_cut", [P, 1]), sb("e_last", [P, 1])
        bias_b = sb("bias_b", [P, D])
        mask3, cum = sb("mask3", [P, T, N]), sb("cum", [P, T, N])
        rank = sb("rank", [P, T, N])
        row_tot, row_base, row_end = sb("row_tot", [P, T]), sb("row_base", [P, T]), sb("row_end", [P, T])
        before, ones = sb("before", [P, P]), sb("ones", [P, P])
        t_row, t_one = sb("t_row", [P, P]), sb("t_one", [P, 1])
        ended, sel = sb("ended", [P, T, P]), sb("sel", [P, T, P])
        at_col, selT = sb("at_col", [P, N]), sb("selT", [P, T, P])
        late, not_edge = sb("late", [P, T, N]), sb("not_edge", [P, T, N])
        att_a, att_b = sb("att_a", [P, T, N]), sb("att_b", [P, T, N])
        a_max, a_neg, a_sum, a_inv = (sb(f"a_{n}", [P, T]) for n in ("max", "neg", "sum", "inv"))
        a_exp, a3 = sb("a_exp", [P, T, N]), sb("a3", [P, T, N])
        diag_t, a_diag = sb("diag_t", [P, T, P]), sb("a_diag", [P, T])
        a_off = sb("a_off", [P, T, N])
        a_offT = sb("a_offT", [P, T, N])
        h1 = sb("h1", [P, TG, D])
        h0 = sb("h0", [P, TG, D])
        h0_bias = sb("h0_bias", [P, TG, D])

        bank = [[ctx.enter_context(nc.psum_tensor(f"bank{n}{c}", [P, CH], fp32)) for c in "ab"]
                for n in range(LAYERS)]

        def tiles(ap, n=TG):
            return ap.rearrange("p (t d) -> p t d", t=n)

        s_x, s_out = sem("x_loaded"), sem("out_stored")
        s_adj, s_qkv, s_w1, s_l2w, s_l3w = (sem(f"loaded_{n}") for n in ("adj", "qkv", "w1", "l2", "l3"))
        s_half, s_ident = sem("minus_half_set"), sem("ident_set")
        s_consts = sem("consts_set")
        stats_seen = per_layer("stats_seen")
        meanvar_ok = per_layer("meanvar_ok")
        var_eps_ok = per_layer("var_eps_ok")
        rstd_ok = per_layer("rstd_ok")
        xn_ok = per_layer("xn_ok")
        t_done = per_layer("t_done")
        hT_ok = per_layer("hT_ok")

        g_done, hv_done = sem("g_done"), sem("hv_done")
        gT_ok, hv_ok = sem("gT_ok"), sem("hv_ok")
        score_done = [sem(f"score_done{b}") for b in range(GB)]
        tanh_ok = [sem(f"tanh_ok{b}") for b in range(GB)]
        exp_ok = [sem(f"exp_ok{b}") for b in range(GB)]
        pT_ok = [sem(f"pT_ok{b}") for b in range(GB)]
        o_done = [sem(f"o_done{b}") for b in range(GB)]
        row_inv_ok = [sem(f"row_inv_ok{b}") for b in range(GB)]
        x_ok = per_layer("x_ok")
        z_done = [sem(f"z_done{n}") for n in range(HOPS + 1)]
        z_ok = [sem(f"z_ok{n}") for n in range(HOPS)]
        pair_done, hh_done, s_done = sem("pair_done"), sem("hh_done"), sem("s_done")
        t_min_ok, t_lr_ok, e_min_ok, e_lr_ok = sem("t_min_ok"), sem("t_lr_ok"), sem("e_min_ok"), sem("e_lr_ok")
        e_max_ok, j_max_ok, neg_max_ok = sem("e_max_ok"), sem("j_max_ok"), sem("neg_max_ok")
        w_low_ok, p2_ok, low_sum_ok, all_sum_ok, col_inv_ok = (
            sem(f"{n}_ok") for n in ("w_low", "p2", "low_sum", "all_sum", "col_inv"))
        hh_up_ok, hh_low_ok, out2_done = sem("hh_up_ok"), sem("hh_low_ok"), sem("out2_done")
        bias_ok, h1_done, h0_done, h1_ok, h0_ok, x_diag_ok, out3_done = (
            sem(n) for n in ("bias_ok", "h1_done", "h0_done", "h1_ok", "h0_ok", "x_diag_ok", "out3_done"))

        setup = {n: sem(f"setup_{n}") for n in (
            "first_stats",
            "qk_t", "qkT", "m_t", "m_qk", "adj_t", "adjT", "w_hop", "hv_ones",
            "oth_t", "othersT", "u_t", "u_cols", "u_sum", "up1", "up_bound", "low_raw", "any",
            "some", "edgeless", "low_mask", "low_end",
            "mask3", "cum", "row_tot", "base_t", "row_base", "ranked", "rank", "ended", "sel",
            "g_t", "at_col", "sel_t", "selT", "v_t", "late", "att_a", "att_b", "a_max", "a_neg",
            "a_exp", "a_inv", "a3", "diag_t", "a_diag", "a_off", "a_t", "a_offT")}

        x_v = x.rearrange("(g b) (j p) d -> g j p b d", b=GB, p=P)
        out_v = out.rearrange("(g b) (j p) d -> g j p b d", b=GB, p=P)

        block = ctx.enter_context(nc.Block())

        @block.sync
        def _(sp):
            for jt in range(T):
                sp.dma_start(x_all[:, 0, jt * GB:(jt + 1) * GB, :], x_v[0, jt]).then_inc(s_x, 16)
            sp.dma_start(w_raw[:], w_cheb).then_inc(s_w1, 16)
            with sp.Fori(1, NG) as g:
                sp.wait_ge(s_x, g * 32)
                for jt in range(T):
                    sp.dma_start(x_all[:, g, jt * GB:(jt + 1) * GB, :], x_v[g, jt]).then_inc(s_x, 16)
            with sp.Fori(0, NG) as g:
                sp.wait_ge(x_ok[3], g + 1)
                for jt in range(T):
                    sp.dma_start(out_v[g, jt], x_all[:, g, jt * GB:(jt + 1) * GB, :]).then_inc(s_out, 16)
            sp.wait_ge(s_out, NG * T * 16)

        @block.gpsimd
        def _(pool):
            nc.gpsimd.memset(ident[:], 0.0).then_inc(s_ident, 1)
            nc.gpsimd.memset(minus_half[:], -0.5).then_inc(s_half, 1)
            nc.gpsimd.memset(eps_t[:], EPS).then_inc(s_half, 1)
            pool.wait_ge(s_ident, 1)
            nc.gpsimd.affine_select(out=ident[:], in_=ident[:], compare_op=ALU.not_equal, fill=1.0,
                                    base=0, pattern=[[-1, P]], channel_multiplier=1).then_inc(s_ident, 1)
            nc.gpsimd.memset(hv1[:, :, D:D + 1], 1.0).then_inc(setup["hv_ones"], 1)

            def inv_std(n, g):
                pool.wait_ge(meanvar_ok[n], g + 1)
                nc.gpsimd.tensor_tensor(var_eps[n][:], meanvar[n][:, :, 1], eps_t[:], ALU.add).then_inc(var_eps_ok[n], 1)
                pool.wait_ge(var_eps_ok[n], g + 1)
                nc.gpsimd.tensor_tensor(rstd[n][:], var_eps[n][:], minus_half[:], ALU.pow).then_inc(rstd_ok[n], 1)

            pool.wait_ge(s_half, 2)
            inv_std(0, 0)
            pool.wait_ge(s_w1, 16)
            nc.gpsimd.tensor_copy(w_hop[:, 0, :], w_raw[:, :, 0])
            for n in range(1, HOPS + 1):
                last = nc.gpsimd.tensor_tensor(w_hop[:, n, :], w_raw[:, :, n], w_raw[:, :, n + HOPS], ALU.add)
            last.then_inc(setup["w_hop"], 1)
            nc.gpsimd.memset(ones[:], 1.0).then_inc(s_consts, 1)
            pool.wait_ge(s_consts, 1)
            nc.gpsimd.affine_select(out=before[:], in_=ones[:], compare_op=ALU.is_gt, fill=0.0, base=0,
                                    pattern=[[1, P]], channel_multiplier=-1)
            nc.gpsimd.iota(t_row[:], pattern=[[1, P]], base=0, channel_multiplier=0,
                           allow_small_or_imprecise_dtypes=True)
            nc.gpsimd.iota(t_one[:], pattern=[[0, 1]], base=1, channel_multiplier=1,
                           allow_small_or_imprecise_dtypes=True)
            pool.wait_ge(s_l3w, 4 * 16)
            nc.gpsimd.affine_select(out=e_cut[:], in_=e_col[:], compare_op=ALU.not_equal, fill=0.0,
                                    base=-(NE - 1), pattern=[[0, 1]], channel_multiplier=1).then_inc(s_consts, 1)
            def off_diagonal():
                pool.wait_ge(setup["a3"], 1)
                for it in range(T):
                    nc.gpsimd.affine_select(out=a_off[:, it, :], in_=a3[:, it, :], compare_op=ALU.not_equal, fill=0.0,
                                            base=it * P, pattern=[[-1, N]],
                                            channel_multiplier=1).then_inc(setup["a_off"], 1)

            def body(s, layers):
                if 2 in layers:
                    inv_std(2, s - 2)
                if 0 in layers and not (isinstance(s, int) and s == NG - 1):
                    inv_std(0, s + 1)
                if 2 in layers:
                    pool.wait_ge(hh_up_ok, s - 1)
                    nc.gpsimd.tensor_tensor(hh_low[:], hh_up[:], w_low[:].unsqueeze(2).broadcast_to([P, TG, D]),
                                            ALU.mult).then_inc(hh_low_ok, 1)
                if 3 in layers:
                    pool.wait_ge(h0_ok, s - 2)
                    nc.gpsimd.tensor_tensor(h0_bias[:], h0[:], bias_b[:].unsqueeze(1).broadcast_to([P, TG, D]),
                                            ALU.add).then_inc(bias_ok, 1)
                if 0 in layers:
                    inv_std(1, s)
                if 2 in layers:
                    inv_std(3, s - 2)

            body(0, range(1))
            body(1, range(2))
            off_diagonal()
            body(2, range(3))
            with pool.Fori(LAYERS - 1, NG - 1) as s:
                body(s, range(LAYERS))
            body(NG - 1, range(LAYERS))
            for s in range(NG, NG + LAYERS - 1):
                body(s, range(s - NG + 1, LAYERS))

        @block.scalar
        def _(act):
            act.dma_start(q_nat[:], q).then_inc(s_qkv, 16)
            act.dma_start(k_nat[:], k).then_inc(s_qkv, 16)
            act.dma_start(adj_nat[:], adj.rearrange("(t p) j -> p t j", p=P)).then_inc(s_adj, 16)
            act.dma_start(v_sb[:], v).then_inc(s_qkv, 16)
            act.dma_start(others[:], w_others).then_inc(s_l2w, 16)
            act.dma_start(w_selfs[:], w_self).then_inc(s_l2w, 16)
            act.dma_start(att_cols[:], w_att.rearrange("(c p) a -> p (c a)", p=P),
                          allow_slow_non_contiguous=True).then_inc(s_l2w, 16)
            act.dma_start(w01[:], w_pair.rearrange("c f g -> f c g")).then_inc(s_l3w, 16)
            act.dma_start(e_col[:], e_vals.rearrange("a t -> t a")).then_inc(s_l3w, 16)
            act.dma_start(e_last[:], e_vals[0:1, NE - 1:NE].broadcast_to([P, 1])).then_inc(s_l3w, 16)
            act.dma_start(bias_b[:], bias.rearrange("(a d) -> a d", a=1).broadcast_to([P, D])).then_inc(s_l3w, 16)

            def copy(out_ap, in_ap):
                return nc.scalar.activation(out_ap, in_ap, ACT.Copy)

            act.wait_ge(setup["qk_t"], 1)
            copy(qkT[:], tiles(bank[1][0][:, 0:2 * D], 2)).then_inc(setup["qkT"], 1)
            act.wait_ge(setup["m_t"], 1)
            copy(m_qk[:], bank[1][1][:, 0:D]).then_inc(setup["m_qk"], 1)

            def relu_t(n, g):
                act.wait_ge(t_done[n], g + 1)
                nc.scalar.activation(hT[n][:], tiles(bank[n][1 if n == 1 else 0][:]), ACT.Relu).then_inc(hT_ok[n], 1)

            relu_t(0, 0)
            def setup_exp():
                act.wait_ge(setup["a_neg"], 1)
                for it in range(T):
                    nc.scalar.activation(a_exp[:, it, :], att_b[:, it, :], ACT.Exp, bias=a_neg[:, it:it + 1],
                                         accum_out=a_sum[:, it:it + 1]).then_inc(setup["a_exp"], 1)

            def body(s, layers):
                if 0 in layers:
                    act.wait_ge(g_done, s + 1)
                    copy(gT[:], tiles(bank[0][1][:])).then_inc(gT_ok, 1)
                if 1 in layers:
                    act.wait_ge(z_done[3], s)
                    copy(z[2][:], tiles(bank[1][0][:])).then_inc(z_ok[2], 1)
                if 0 in layers:
                    for b in range(GB):
                        act.wait_ge(score_done[b], s + 1)
                        nc.scalar.activation(tanh_s[:, b], tiles(bank[0][1 - b][:], T), ACT.Tanh,
                                             scale=SCORE_SCALE).then_inc(tanh_ok[b], 1)
                if 2 in layers:
                    relu_t(2, s - 2)
                if 0 in layers:
                    for b in range(GB):
                        act.wait_ge(tanh_ok[b], s + 1)
                        nc.scalar.activation(exp_s[:, b], tanh_s[:, b], ACT.Exp, scale=8.0).then_inc(exp_ok[b], 1)
                if 1 in layers:
                    act.wait_ge(z_done[2], s)
                    copy(z[1][:], tiles(bank[1][1][:])).then_inc(z_ok[1], 1)
                if 2 in layers:
                    g = s - 2
                    act.wait_ge(neg_max_ok, g + 1)
                    nc.scalar.activation(w_low[:], t_diff[:], ACT.Exp).then_inc(w_low_ok, 1)
                    for t in range(TG):
                        last = nc.scalar.activation(p2[:, t, :], e_lr[:, t, :], ACT.Exp, bias=neg_max[:, t:t + 1],
                                                    accum_out=up_sum[:, t:t + 1])
                    last.then_inc(p2_ok, 1)
                if 1 in layers:
                    act.wait_ge(z_done[1], s)
                    copy(z[0][:], tiles(bank[1][0][:])).then_inc(z_ok[0], 1)
                if 3 in layers:
                    g = s - 3
                    act.wait_ge(h1_done, g + 1)
                    copy(h1[:], tiles(bank[3][1][:])).then_inc(h1_ok, 1)
                    act.wait_ge(h0_done, g + 1)
                    for it in range(T):
                        c = it * GB
                        last = nc.scalar.activation(h0[:, c:c + GB, :], tiles(bank[3][0][:])[:, c:c + GB, :],
                                                    ACT.Copy, scale=a_diag[:, it:it + 1])
                    last.then_inc(h0_ok, 1)
                if 0 in layers:
                    if not (isinstance(s, int) and s == NG - 1):
                        relu_t(0, s + 1)
                    relu_t(1, s)
                if 2 in layers:
                    relu_t(3, s - 2)

            body(0, range(1))
            body(1, range(2))
            setup_exp()
            body(2, range(3))
            with act.Fori(LAYERS - 1, NG - 1) as s:
                body(s, range(LAYERS))
            body(NG - 1, range(LAYERS))
            for s in range(NG, NG + LAYERS - 1):
                body(s, range(s - NG + 1, LAYERS))

        @block.vector
        def _(dve):
            def wait_alone(s, n):
                dve.wait_ge(s_x, 32)
                dve.wait_ge(s, n)

            def moments(n, g, ready, count):
                wait_alone(ready, count)
                for t in range(TG):
                    last = nc.vector.bn_stats(stats[n][:, t, :], x_all[:, g, t, :])
                first = n == 0 and isinstance(g, int) and g == 0
                seen, at = (setup["first_stats"], 1) if first else (stats_seen[n], g if n == 0 else g + 1)
                last.then_inc(seen, 1)
                wait_alone(seen, at)
                for t in range(TG):
                    last = nc.vector.bn_aggr(meanvar[n][:, t, :], stats[n][:, t, :])
                last.then_inc(meanvar_ok[n], 1)

            def normalise(n, g):
                dve.wait_ge(rstd_ok[n], g + 1)
                for t in range(TG):
                    last = nc.vector.tensor_scalar(xn[n][:, t, :], x_all[:, g, t, :], meanvar[n][:, t, 0:1],
                                                   rstd[n][:, t:t + 1], ALU.subtract, ALU.mult)
                last.then_inc(xn_ok[n], 1)

            moments(0, 0, s_x, 32)
            normalise(0, 0)
            dve.wait_ge(setup["adj_t"], 1)
            nc.vector.tensor_copy(adjT[:], tiles(bank[0][1][:], T)).then_inc(setup["adjT"], 1)

            def setup_layer2():
                dve.wait_ge(setup["oth_t"], 1)
                nc.vector.tensor_copy(othersT[:], bank[2][0][:, 0:D]).then_inc(setup["othersT"], 1)
                dve.wait_ge(setup["adjT"], 1)
                nc.vector.tensor_scalar(up_bound[:], adjT[:, :, 0:P], 0.0, HUGE, ALU.is_gt,
                                        ALU.mult).then_inc(setup["up1"], 1)
                nc.vector.tensor_scalar(low_mask[:], adjT[:, :, P:N], 0.0, None,
                                        ALU.is_gt).then_inc(setup["low_raw"], 1)
                dve.wait_ge(setup["up1"], 1)
                nc.vector.tensor_reduce(any_up[:], up_bound[:], axis=AX.X, op=ALU.max)
                dve.wait_ge(setup["low_raw"], 1)
                nc.vector.tensor_reduce(any_low[:], low_mask[:], axis=AX.X, op=ALU.max).then_inc(setup["any"], 1)
                dve.wait_ge(setup["any"], 1)
                nc.vector.tensor_tensor(edgeless[:], any_up[:], any_low[:], ALU.max).then_inc(setup["some"], 1)
                nc.vector.tensor_scalar(low_bound[:], any_low[:], HUGE, NEG_PRE, ALU.mult, ALU.add)
                nc.vector.tensor_scalar(up_bound[:], up_bound[:], NEG_PRE, None,
                                        ALU.add).then_inc(setup["up_bound"], 1)
                dve.wait_ge(setup["some"], 1)
                nc.vector.tensor_scalar(edgeless[:], edgeless[:], 0.0, None,
                                        ALU.is_le).then_inc(setup["edgeless"], 1)
                dve.wait_ge(setup["edgeless"], 1)
                for jt in range(T):
                    last = nc.vector.tensor_scalar(low_mask[:, jt, :], low_mask[:, jt, :], edgeless[:, jt:jt + 1],
                                                   None, ALU.max)
                last.then_inc(setup["low_mask"], 1)
                dve.wait_ge(setup["low_mask"], 1)
                nc.vector.tensor_reduce(low_count[:], low_mask[:], axis=AX.X, op=ALU.add).then_inc(setup["low_end"], 1)
                dve.wait_ge(setup["u_t"], 1)
                nc.vector.tensor_copy(u_cols[:], bank[2][1][:, 0:2]).then_inc(setup["u_cols"], 1)
                dve.wait_ge(setup["u_cols"], 1)
                nc.vector.tensor_scalar(u_sum[:], u_cols[:, 0:1].broadcast_to([P, P]), u_cols[:, 1:2], None,
                                        ALU.add).then_inc(setup["u_sum"], 1)

            def setup_layer3():
                def cf(n):
                    return setup[n]
                dve.wait_ge(s_adj, 16)
                nc.vector.tensor_scalar(mask3[:], adj_nat[:], 0.0, None, ALU.is_gt).then_inc(cf("mask3"), 1)
                dve.wait_ge(cf("mask3"), 1)
                for it in range(T):
                    last = nc.vector.tensor_tensor_scan(cum[:, it, :], mask3[:, it, :], mask3[:, it, :], 0.0,
                                                        ALU.add, ALU.max)
                last.then_inc(cf("cum"), 1)
                dve.wait_ge(cf("cum"), 1)
                nc.vector.tensor_copy(row_tot[:], cum[:, :, N - 1]).then_inc(cf("row_tot"), 1)
                nc.vector.tensor_scalar(not_edge[:], mask3[:], 1.0, -NEG, ALU.subtract, ALU.mult)
                dve.wait_ge(cf("base_t"), 1)
                nc.vector.tensor_copy(row_base[:], bank[3][0][:, 0:T]).then_inc(cf("row_base"), 1)
                dve.wait_ge(cf("row_base"), 1)
                nc.vector.tensor_tensor(row_end[:], row_base[:], row_tot[:], ALU.add).then_inc(cf("row_base"), 1)
                for it in range(T):
                    last = nc.vector.scalar_tensor_tensor(rank[:, it, :], cum[:, it, :], row_base[:, it:it + 1],
                                                          mask3[:, it, :], ALU.add, ALU.mult)
                last.then_inc(cf("rank"), 1)
                dve.wait_ge(s_consts, 2)
                dve.wait_ge(cf("row_base"), 2)
                for it in range(T):
                    last = nc.vector.tensor_scalar(ended[:, it, :], t_row[:], row_end[:, it:it + 1], None, ALU.is_lt)
                last.then_inc(cf("ended"), 1)
                dve.wait_ge(cf("ended"), 1)
                for it in range(T):
                    last = nc.vector.scalar_tensor_tensor(sel[:, it, :], t_row[:], row_base[:, it:it + 1],
                                                          ended[:, it, :], ALU.is_ge, ALU.mult)
                last.then_inc(cf("sel"), 1)
                dve.wait_ge(cf("rank"), 1)
                nc.vector.tensor_scalar(late[:], rank[:], float(NE), e_last[:, 0:1], ALU.is_ge,
                                        ALU.mult).then_inc(cf("late"), 1)
                dve.wait_ge(cf("g_t"), 1)
                nc.vector.tensor_scalar(at_col[:], bank[3][0][:, 0:N], t_one[:, 0:1], None,
                                        ALU.is_equal).then_inc(cf("at_col"), 1)
                dve.wait_ge(cf("sel_t"), 1)
                nc.vector.tensor_scalar(selT[:], tiles(bank[3][1][:, 0:N], T), e_cut[:, 0:1], None,
                                        ALU.mult).then_inc(cf("selT"), 1)
                dve.wait_ge(cf("v_t"), 1)
                dve.wait_ge(cf("late"), 1)
                nc.vector.tensor_tensor(att_a[:], tiles(bank[3][0][:], T), late[:], ALU.add).then_inc(cf("att_a"), 1)
                dve.wait_ge(cf("att_a"), 1)
                nc.vector.tensor_tensor(att_b[:], att_a[:], not_edge[:], ALU.add).then_inc(cf("att_b"), 1)
                dve.wait_ge(cf("att_b"), 1)
                nc.vector.tensor_reduce(a_max[:], att_b[:], axis=AX.X, op=ALU.max).then_inc(cf("a_max"), 1)
                dve.wait_ge(cf("a_max"), 1)
                nc.vector.tensor_scalar(a_neg[:], a_max[:], -1.0, None, ALU.mult).then_inc(cf("a_neg"), 1)
                dve.wait_ge(cf("a_exp"), T)
                nc.vector.reciprocal(a_inv[:], a_sum[:]).then_inc(cf("a_inv"), 1)
                dve.wait_ge(cf("a_inv"), 1)
                for it in range(T):
                    last = nc.vector.tensor_scalar(a3[:, it, :], a_exp[:, it, :], a_inv[:, it:it + 1], None, ALU.mult)
                last.then_inc(cf("a3"), 1)
                dve.wait_ge(cf("a3"), 1)
                for it in range(T):
                    last = nc.vector.tensor_tensor(diag_t[:, it, :], a3[:, it, it * P:(it + 1) * P], ident[:], ALU.mult)
                last.then_inc(cf("diag_t"), 1)
                dve.wait_ge(cf("diag_t"), 1)
                nc.vector.tensor_reduce(a_diag[:], diag_t[:], axis=AX.X, op=ALU.add).then_inc(cf("a_diag"), 1)
                dve.wait_ge(cf("a_t"), 1)
                nc.vector.tensor_copy(a_offT[:], tiles(bank[3][0][:], T)).then_inc(cf("a_offT"), 1)
                dve.wait_ge(cf("a_diag"), 1)

            def add_to_x(n, g, src):
                nc.vector.tensor_tensor(x_all[:, g], tiles(src[:]), x_all[:, g], ALU.add).then_inc(x_ok[n], 1)

            def pair_scores(g):
                dve.wait_ge(pair_done, g + 1)
                nc.vector.tensor_tensor(t_min[:].rearrange("p (j b) -> p j b", j=T),
                                        bank[2][1][:, 0:GB].unsqueeze(1).broadcast_to([P, T, GB]),
                                        low_bound[:].unsqueeze(2).broadcast_to([P, T, GB]),
                                        ALU.min).then_inc(t_min_ok, 1)
                dve.wait_ge(t_min_ok, g + 1)
                nc.vector.scalar_tensor_tensor(t_lr[:], t_min[:], SLOPE, t_min[:], ALU.mult,
                                               ALU.max).then_inc(t_lr_ok, 1)
                dve.wait_ge(s_done, g + 1)
                nc.vector.tensor_tensor(e_min[:].rearrange("p (j b) i -> p j b i", j=T),
                                        bank[2][1][:].rearrange("p (j b i) -> p j b i", j=T, b=GB),
                                        up_bound[:].unsqueeze(2).broadcast_to([P, T, GB, P]),
                                        ALU.min).then_inc(e_min_ok, 1)
                dve.wait_ge(e_min_ok, g + 1)
                nc.vector.scalar_tensor_tensor(e_lr[:], e_min[:], SLOPE, e_min[:], ALU.mult,
                                               ALU.max).then_inc(e_lr_ok, 1)
                dve.wait_ge(e_lr_ok, g + 1)
                nc.vector.tensor_reduce(e_max[:], e_lr[:], axis=AX.X, op=ALU.max).then_inc(e_max_ok, 1)
                dve.wait_ge(e_max_ok, g + 1)
                dve.wait_ge(t_lr_ok, g + 1)
                nc.vector.tensor_tensor(j_max[:], e_max[:], t_lr[:], ALU.max).then_inc(j_max_ok, 1)
                dve.wait_ge(j_max_ok, g + 1)
                nc.vector.tensor_tensor(t_diff[:], t_lr[:], j_max[:], ALU.subtract)
                nc.vector.tensor_scalar(neg_max[:], j_max[:], -1.0, None, ALU.mult).then_inc(neg_max_ok, 1)

            def pair_sums(g):
                dve.wait_ge(w_low_ok, g + 1)
                nc.vector.tensor_tensor(low_sum[:].rearrange("p (j b) -> p j b", j=T),
                                        w_low[:].rearrange("p (j b) -> p j b", j=T),
                                        low_count[:].unsqueeze(2).broadcast_to([P, T, GB]),
                                        ALU.mult).then_inc(low_sum_ok, 1)
                dve.wait_ge(low_sum_ok, g + 1)
                dve.wait_ge(p2_ok, g + 1)
                nc.vector.tensor_tensor(all_sum[:], low_sum[:], up_sum[:], ALU.add).then_inc(all_sum_ok, 1)
                dve.wait_ge(all_sum_ok, g + 1)
                nc.vector.reciprocal(col_inv[:], all_sum[:]).then_inc(col_inv_ok, 1)
                dve.wait_ge(col_inv_ok, g + 1)
                dve.wait_ge(hh_done, g + 1)
                nc.vector.tensor_tensor(hh_up[:], tiles(bank[2][0][:]),
                                        col_inv[:].unsqueeze(2).broadcast_to([P, TG, D]),
                                        ALU.mult).then_inc(hh_up_ok, 1)

            def body(s, layers):
                if 2 in layers:
                    moments(2, s - 2, x_ok[1], s - 1)
                if 0 in layers:
                    dve.wait_ge(hv_done, s + 1)
                    nc.vector.tensor_copy(hv1[:, :, 0:D], tiles(bank[0][0][:])).then_inc(hv_ok, 1)
                    if not (isinstance(s, int) and s == NG - 1):
                        moments(0, s + 1, s_x, s * 32 + 64)
                if 2 in layers:
                    normalise(2, s - 2)
                if 0 in layers:
                    if not (isinstance(s, int) and s == NG - 1):
                        normalise(0, s + 1)
                    for b in range(GB):
                        dve.wait_ge(exp_ok[b], s + 1)
                        nc.vector.tensor_tensor(pT[:, b], exp_s[:, b], adjT[:], ALU.mult).then_inc(pT_ok[b], 1)
                if 2 in layers:
                    pair_scores(s - 2)
                    pair_sums(s - 2)
                if 0 in layers:
                    for b in range(GB):
                        dve.wait_ge(o_done[b], s + 1)
                        o = bank[0][1 - b][:, 0:T * (D + 1)].rearrange("p (i d) -> p i d", i=T)
                        nc.vector.reciprocal(row_inv[:, b, :], o[:, :, D]).then_inc(row_inv_ok[b], 1)
                        dve.wait_ge(row_inv_ok[b], s + 1)
                        for it in range(T):
                            t = it * GB + b
                            last = nc.vector.scalar_tensor_tensor(x_all[:, s, t, :], o[:, it, 0:D],
                                                                  row_inv[:, b, it:it + 1], x_all[:, s, t, :],
                                                                  ALU.mult, ALU.add)
                    last.then_inc(x_ok[0], 1)
                    moments(1, s, x_ok[0], s + 1)
                if 2 in layers:
                    dve.wait_ge(out2_done, s - 1)
                    add_to_x(2, s - 2, bank[2][1])
                    moments(3, s - 2, x_ok[2], s - 1)
                if 0 in layers:
                    normalise(1, s)
                if 3 in layers:
                    g = s - 3
                    dve.wait_ge(bias_ok, g + 1)
                    nc.vector.tensor_tensor(x_all[:, g], h0_bias[:], x_all[:, g], ALU.add).then_inc(x_diag_ok, 1)
                if 2 in layers:
                    normalise(3, s - 2)
                if 3 in layers:
                    dve.wait_ge(out3_done, g + 1)
                    dve.wait_ge(x_diag_ok, g + 1)
                    add_to_x(3, g, bank[3][1])
                if 1 in layers:
                    dve.wait_ge(z_done[0], s)
                    add_to_x(1, s - 1, bank[1][0])

            body(0, range(1))
            setup_layer2()
            body(1, range(2))
            setup_layer3()
            body(2, range(3))
            with dve.Fori(LAYERS - 1, NG - 1) as s:
                body(s, range(LAYERS))
            body(NG - 1, range(LAYERS))
            for s in range(NG, NG + LAYERS - 1):
                body(s, range(s - NG + 1, LAYERS))

        @block.tensor
        def _(pe):
            def mm(o, lhsT, rhs, start=True, stop=True, shared=False):
                return nc.tensor.matmul(o, lhsT, rhs, start=start, stop=stop, skip_group_check=shared)

            def transposes(n, g):
                pe.wait_ge(xn_ok[n], g + 1)
                bk = tiles(bank[n][1 if n == 1 else 0][:])
                for t in range(TG):
                    to = t % GB * T + t // GB if n == 2 else t
                    last = nc.tensor.transpose(bk[:, to, :], xn[n][:, t, :], ident[:])
                last.then_inc(t_done[n], 1)

            pe.wait_ge(s_ident, 2)
            pe.wait_ge(s_qkv, 48)
            bk = tiles(bank[1][0][:, 0:2 * D], 2)
            nc.tensor.transpose(bk[:, 0, :], q_nat[:], ident[:])
            nc.tensor.transpose(bk[:, 1, :], k_nat[:], ident[:]).then_inc(setup["qk_t"], 1)
            pe.wait_ge(s_adj, 16)
            bk = tiles(bank[0][1][:], T)
            for it in range(T):
                for jt in range(T):
                    last = nc.tensor.transpose(bk[:, jt, it * P:(it + 1) * P], adj_nat[:, it, jt * P:(jt + 1) * P],
                                               ident[:])
            last.then_inc(setup["adj_t"], 1)
            pe.wait_ge(setup["qkT"], 1)
            mm(bank[1][1][:, 0:D], qkT[:, 0, :], qkT[:, 1, :]).then_inc(setup["m_t"], 1)
            transposes(0, 0)

            for n in ("adjT", "m_qk", "hv_ones"):
                pe.wait_ge(setup[n], 1)

            def setup_layer2():
                pe.wait_ge(s_l2w, 48)
                nc.tensor.transpose(bank[2][0][:, 0:D], others[:], ident[:]).then_inc(setup["oth_t"], 1)
                pe.wait_ge(setup["othersT"], 1)
                mm(bank[2][1][:, 0:2], othersT[:], att_cols[:]).then_inc(setup["u_t"], 1)
                for n in ("u_sum", "low_mask"):
                    pe.wait_ge(setup[n], 1)

            def setup_layer3():
                pe.wait_ge(setup["row_tot"], 1)
                pe.wait_ge(s_consts, 2)
                mm(bank[3][0][:, 0:1], before[:], row_tot[:, 0:1])
                mm(bank[3][0][:, 1:2], ones[:], row_tot[:, 0:1], stop=False)
                mm(bank[3][0][:, 1:2], before[:], row_tot[:, 1:2], start=False).then_inc(setup["base_t"], 1)
                pe.wait_ge(setup["sel"], 1)
                pe.wait_ge(setup["rank"], 1)
                pe.wait_ge(setup["row_base"], 1)
                for it in range(T):
                    last = mm(bank[3][0][:, 0:N], sel[:, it, :], rank[:, it, :], start=it == 0, stop=it == T - 1)
                last.then_inc(setup["g_t"], 1)
                for it in range(T):
                    last = nc.tensor.transpose(bank[3][1][:, it * P:(it + 1) * P], sel[:, it, :], ident[:])
                last.then_inc(setup["sel_t"], 1)
                pe.wait_ge(setup["at_col"], 1)
                pe.wait_ge(setup["selT"], 1)
                for it in range(T):
                    last = mm(bank[3][0][:, it * N:(it + 1) * N], selT[:, it, :], at_col[:])
                last.then_inc(setup["v_t"], 1)
                pe.wait_ge(setup["a_off"], T)
                pe.wait_ge(setup["att_a"], 1)
                bk = tiles(bank[3][0][:], T)
                for it in range(T):
                    for jt in range(T):
                        last = nc.tensor.transpose(bk[:, jt, it * P:(it + 1) * P], a_off[:, it, jt * P:(jt + 1) * P],
                                                   ident[:])
                last.then_inc(setup["a_t"], 1)
                pe.wait_ge(setup["a_offT"], 1)

            def bank_read(s, n):
                if not isinstance(n, int) or n > 0:
                    pe.wait_ge(s, n)

            def horner(bk, hop, prev):
                o = tiles(bk[:])
                for it in range(T):
                    c = it * GB
                    for b in range(GB):
                        last = mm(o[:, c + b, :], hT[1][:, c + b, :], w_hop[:, hop, :], start=b == 0,
                                  stop=prev is None, shared=True)
                    if prev is not None:
                        for jt in range(T):
                            last = mm(o[:, c:c + GB, :], adjT[:, jt, it * P:(it + 1) * P],
                                      prev[:, jt * GB:(jt + 1) * GB, :], start=False, stop=jt == T - 1, shared=True)
                last.then_inc(z_done[hop], 1)

            def body(s, layers):
                if 0 in layers:
                    pe.wait_ge(hT_ok[0], s + 1)
                    mm(bank[0][1][:], m_qk[:], hT[0][:].rearrange("p t d -> p (t d)")).then_inc(g_done, 1)
                    for t in range(TG):
                        last = mm(tiles(bank[0][0][:])[:, t, :], hT[0][:, t, :], v_sb[:])
                    last.then_inc(hv_done, 1)
                if 1 in layers:
                    pe.wait_ge(hT_ok[1], s)
                    bank_read(x_ok[1], s - 1)
                    horner(bank[1][0], HOPS, None)
                if 0 in layers:
                    pe.wait_ge(gT_ok, s + 1)
                    pe.wait_ge(hv_ok, s + 1)
                    gv = gT[:].rearrange("p (i b) d -> p i b d", b=GB)
                    for b in range(GB):
                        for jt in range(T):
                            last = mm(tiles(bank[0][1 - b][:], T)[:, jt, :].rearrange("p (i d) -> p i d", i=T),
                                      hT[0][:, jt * GB + b, :], gv[:, :, b, :])
                        last.then_inc(score_done[b], 1)
                if 2 in layers:
                    transposes(2, s - 2)
                if 1 in layers:
                    pe.wait_ge(z_ok[2], s)
                    horner(bank[1][1], 2, z[2])
                if 2 in layers:
                    g = s - 2
                    pe.wait_ge(hT_ok[2], g + 1)
                    bank_read(x_ok[2], g)
                    pairs = hT[2][:].rearrange("p (b i) (c r) -> p r b (i c)", b=GB, r=2)
                    for b in range(GB):
                        for r in range(2):
                            last = mm(bank[2][1][:, b:b + 1], pairs[:, r, b, :], u_cols[:, r:r + 1],
                                      start=r == 0, stop=r == 1)
                    last.then_inc(pair_done, 1)
                    for t in range(TG):
                        last = mm(tiles(bank[2][0][:])[:, t, :], hT[2][:, t % GB * T + t // GB, :], others[:])
                    last.then_inc(hh_done, 1)
                    pe.wait_ge(t_min_ok, g + 1)
                    mm(bank[2][1][:].rearrange("p (j b i) -> p j b i", j=T, b=GB), u_sum[:], pairs).then_inc(s_done, 1)
                if 1 in layers:
                    pe.wait_ge(z_ok[1], s)
                    horner(bank[1][0], 1, z[1])
                if 3 in layers:
                    g = s - 3
                    pe.wait_ge(hT_ok[3], g + 1)
                    bank_read(x_ok[3], g)
                    for t in range(TG):
                        last = mm(tiles(bank[3][1][:])[:, t, :], hT[3][:, t, :], w01[:, 1, :])
                    last.then_inc(h1_done, 1)
                    for t in range(TG):
                        last = mm(tiles(bank[3][0][:])[:, t, :], hT[3][:, t, :], w01[:, 0, :])
                    last.then_inc(h0_done, 1)
                if 0 in layers:
                    for b in range(GB):
                        pe.wait_ge(pT_ok[b], s + 1)
                        o = bank[0][1 - b][:, 0:T * (D + 1)].rearrange("p (i d) -> p i d", i=T)
                        for it in range(T):
                            for jt in range(T):
                                last = mm(o[:, it, :], pT[:, b, jt, it * P:(it + 1) * P], hv1[:, jt * GB + b, :],
                                          start=jt == 0, stop=jt == T - 1)
                        last.then_inc(o_done[b], 1)
                if 2 in layers:
                    g = s - 2
                    o = tiles(bank[2][1][:])
                    pe.wait_ge(p2_ok, g + 1)
                    pe.wait_ge(e_min_ok, g + 1)
                    pe.wait_ge(hh_up_ok, g + 1)
                    for b in range(GB):
                        mm(o[:, b, :], hT[2][:, b * T, :], w_selfs[:], stop=False)
                        for jt in range(T):
                            mm(o[:, b, :], p2[:, jt * GB + b, :], hh_up[:, jt * GB + b, :], start=False,
                               stop=jt == T - 1)
                    pe.wait_ge(hh_low_ok, g + 1)
                    for b in range(GB):
                        mm(o[:, GB + b, :], hT[2][:, b * T + 1, :], w_selfs[:], start=b == 0, stop=False, shared=True)
                    for jt in range(T):
                        last = mm(o[:, GB:2 * GB, :], low_mask[:, jt, :], hh_low[:, jt * GB:(jt + 1) * GB, :],
                                  start=False, stop=jt == T - 1, shared=True)
                    last.then_inc(out2_done, 1)
                if 3 in layers:
                    g = s - 3
                    o = tiles(bank[3][1][:])
                    pe.wait_ge(h1_ok, g + 1)
                    for it in range(T):
                        for jt in range(T):
                            last = mm(o[:, it * GB:(it + 1) * GB, :], a_offT[:, jt, it * P:(it + 1) * P],
                                      h1[:, jt * GB:(jt + 1) * GB, :], start=jt == 0, stop=jt == T - 1)
                    last.then_inc(out3_done, 1)
                if 0 in layers and not (isinstance(s, int) and s == NG - 1):
                    pe.wait_ge(x_ok[0], s + 1)
                    transposes(0, s + 1)
                if 1 in layers:
                    pe.wait_ge(z_ok[0], s)
                    horner(bank[1][0], 0, z[0])
                if 0 in layers:
                    transposes(1, s)
                if 2 in layers:
                    if 3 in layers:
                        pe.wait_ge(h0_ok, s - 2)
                    transposes(3, s - 2)

            body(0, range(1))
            pe.wait_ge(setup["w_hop"], 1)
            setup_layer2()
            body(1, range(2))
            setup_layer3()
            body(2, range(3))
            with pe.Fori(LAYERS - 1, NG - 1) as s:
                body(s, range(LAYERS))
            body(NG - 1, range(LAYERS))
            for s in range(NG, NG + LAYERS - 1):
                body(s, range(s - NG + 1, LAYERS))


_INS = ['x', 'adj', 'L0_gnn_q', 'L0_gnn_k', 'L0_gnn_v', 'L1_gnn_weight_1', 'L2_gnn_others_weight',
        'L2_gnn_self_weight', 'L2_gnn_att_weight', 'L3_gnn_W', 'L3_gnn_e', 'L3_gnn_bias']


def kernel(**inputs):
    import numpy as _np
    import concourse.bacc as _bacc
    from concourse import mybir as _mybir
    from concourse.bass_utils import run_bass_kernel_spmd as _run

    nc = _bacc.Bacc("TRN2", target_bir_lowering=False, num_devices=1)
    arrays, args = {}, []
    for name in _INS:
        a = _np.ascontiguousarray(inputs[name])
        arrays[f"in_{name}_dram"] = a
        args.append(nc.dram_tensor(f"in_{name}_dram", a.shape, _mybir.dt.from_np(a.dtype), kind="ExternalInput").ap())
    out = nc.dram_tensor("out_dram", inputs["x"].shape, _mybir.dt.float32, kind="ExternalOutput").ap()
    four_layer_gnn(nc, *args, out)
    r = _run(nc, [arrays], core_ids=[0])
    return r.results[0]["out_dram"]
```

```python
import math
from contextlib import ExitStack

import concourse.bass as bass
from concourse import mybir


def four_layer_gnn(nc, x, adj, q, k, v, w_cheb, w_others, w_self, w_att, w_pair, e_vals, bias, out):
    fp32 = mybir.dt.float32
    f32r = mybir.dt.float32r
    ALU = mybir.AluOpType
    ACT = mybir.ActivationFunctionType
    AX = mybir.AxisListType

    P = 128
    B, N, D = x.shape
    assert D == P and N == 2 * P
    T = N // P
    GB = 2
    NG = B // GB
    TG = T * GB
    CH = TG * D
    LAYERS = 4
    SCORE_SCALE = 1.0 / (8.0 * math.sqrt(D))
    EPS = 1e-5
    SLOPE = 0.1
    NEG = -9.0e15
    NEG_PRE = NEG / SLOPE
    HUGE = 3.0e38
    KW = w_cheb.shape[2]
    HOPS = (KW - 1) // 2
    NE = e_vals.shape[1]
    assert NE == P and NG > LAYERS

    ctx = ExitStack()
    with ctx:
        def sb(name, shape, dt=fp32):
            return ctx.enter_context(nc.sbuf_tensor(name, shape, dt))

        def halves(name, shape):
            return [sb(f"{name}_{n}", shape, f32r) for n in ("hi", "lo")]

        def sem(name):
            return ctx.enter_context(nc.semaphore(name))

        def per_layer(name, layers=range(LAYERS)):
            return {n: sem(f"{name}{n}") for n in layers}

        x_all = sb("x_all", [P, NG, TG, D])
        xn = [sb(f"xn{n}", [P, TG, D]) for n in range(LAYERS)]
        hT = [sb(f"hT{n}", [P, TG, P]) for n in range(LAYERS)]
        stats = [sb(f"stats{n}", [P, TG, 6]) for n in range(LAYERS)]
        meanvar = [sb(f"meanvar{n}", [P, TG, 2]) for n in range(LAYERS)]
        var_eps = [sb(f"var_eps{n}", [P, TG]) for n in range(LAYERS)]
        rstd = [sb(f"rstd{n}", [P, TG]) for n in range(LAYERS)]
        minus_half, eps_t = sb("minus_half", [P, TG]), sb("eps_t", [P, TG])

        ident = sb("ident", [P, P])
        adj_nat = sb("adj_nat", [P, T, N])
        adjT = sb("adjT", [P, T, N])

        q_nat, k_nat, v_sb = sb("q_nat", [P, D]), sb("k_nat", [P, D]), sb("v_sb", [P, D])
        qkT = sb("qkT", [P, 2, D])
        m_qk = sb("m_qk", [P, D])
        gT = sb("gT", [P, TG, P])
        hv1 = sb("hv1", [P, TG, D + 1])
        tanh_s = sb("tanh_s", [P, GB, T, N])
        exp_s = sb("exp_s", [P, GB, T, N])
        pT = sb("pT", [P, GB, T, N])
        row_inv = sb("row_inv", [P, GB, T])

        w_raw = sb("w_raw", [P, D, KW])
        w_hop = sb("w_hop", [P, HOPS + 1, D])
        adjT2 = halves("adjT", [P, T, N])
        z2 = [halves(f"z{n}", [P, TG, D]) for n in range(HOPS)]

        others = sb("others", [P, D])
        w_selfs = sb("w_selfs", [P, D])
        att_cols = sb("att_cols", [P, 2])
        othersT = sb("othersT", [P, D])
        u_cols = sb("u_cols", [P, 2])
        u_sum = sb("u_sum", [P, P])
        up_bound = sb("up_bound", [P, T, P])
        low_mask = sb("low_mask", [P, T, P])
        any_up, any_low, edgeless = sb("any_up", [P, T]), sb("any_low", [P, T]), sb("edgeless", [P, T])
        low_count, low_bound = sb("low_count", [P, T]), sb("low_bound", [P, T])
        e_min = sb("e_min", [P, TG, P])
        e_lr = sb("e_lr", [P, TG, P])
        p2 = sb("p2", [P, TG, P])
        t_min, t_lr = sb("t_min", [P, TG]), sb("t_lr", [P, TG])
        e_max, j_max, neg_max = sb("e_max", [P, TG]), sb("j_max", [P, TG]), sb("neg_max", [P, TG])
        t_diff, w_low, low_sum = sb("t_diff", [P, TG]), sb("w_low", [P, TG]), sb("low_sum", [P, TG])
        up_sum, all_sum, col_inv = sb("up_sum", [P, TG]), sb("all_sum", [P, TG]), sb("col_inv", [P, TG])
        hh_up, hh_low = sb("hh_up", [P, TG, D]), sb("hh_low", [P, TG, D])
        low_mask_r = sb("low_mask_r", [P, T, P], f32r)
        hh_low2 = halves("hh_low", [P, TG, D])

        w01 = sb("w01", [P, 2, D])
        e_col, e_cut, e_last = sb("e_col", [P, 1]), sb("e_cut", [P, 1]), sb("e_last", [P, 1])
        bias_b = sb("bias_b", [P, D])
        mask3, cum = sb("mask3", [P, T, N]), sb("cum", [P, T, N])
        rank = sb("rank", [P, T, N])
        row_tot, row_base, row_end = sb("row_tot", [P, T]), sb("row_base", [P, T]), sb("row_end", [P, T])
        before, ones = sb("before", [P, P]), sb("ones", [P, P])
        t_row, t_one = sb("t_row", [P, P]), sb("t_one", [P, 1])
        ended, sel = sb("ended", [P, T, P]), sb("sel", [P, T, P])
        at_col, selT = sb("at_col", [P, N]), sb("selT", [P, T, P])
        late, not_edge = sb("late", [P, T, N]), sb("not_edge", [P, T, N])
        att_a, att_b = sb("att_a", [P, T, N]), sb("att_b", [P, T, N])
        a_max, a_neg, a_sum, a_inv = (sb(f"a_{n}", [P, T]) for n in ("max", "neg", "sum", "inv"))
        a_exp, a3 = sb("a_exp", [P, T, N]), sb("a3", [P, T, N])
        diag_t = sb("diag_t", [P, T, P])
        a_off = sb("a_off", [P, T, N])
        a_offT = sb("a_offT", [P, T, N])
        a_offT2 = halves("a_offT", [P, T, N])
        h12 = halves("h1", [P, TG, D])
        diag_row = sb("diag_row", [P, T, P])
        hT_diag = sb("hT_diag", [P, TG, P])

        bank = [[ctx.enter_context(nc.psum_tensor(f"bank{n}{c}", [P, CH], fp32)) for c in "ab"]
                for n in range(LAYERS)]

        def tiles(ap, n=TG):
            return ap.rearrange("p (t d) -> p t d", t=n)

        s_x, s_out = sem("x_loaded"), sem("out_stored")
        s_adj, s_qk, s_v, s_w1, s_l2w, s_l3w = (sem(f"loaded_{n}") for n in ("adj", "qk", "v", "w1", "l2", "l3"))
        s_half, s_ident = sem("minus_half_set"), sem("ident_set")
        s_consts = sem("consts_set")
        stats_seen = per_layer("stats_seen")
        meanvar_ok = per_layer("meanvar_ok")
        var_eps_ok = per_layer("var_eps_ok")
        rstd_ok = per_layer("rstd_ok")
        xn_ok = per_layer("xn_ok")
        t_done = per_layer("t_done")
        hT_ok = per_layer("hT_ok")

        g_done, hv_done = sem("g_done"), sem("hv_done")
        gT_ok, hv_ok = sem("gT_ok"), sem("hv_ok")
        score_done = [sem(f"score_done{b}") for b in range(GB)]
        tanh_ok = [sem(f"tanh_ok{b}") for b in range(GB)]
        exp_ok = [sem(f"exp_ok{b}") for b in range(GB)]
        pT_ok = [sem(f"pT_ok{b}") for b in range(GB)]
        o_done = [sem(f"o_done{b}") for b in range(GB)]
        row_inv_ok = [sem(f"row_inv_ok{b}") for b in range(GB)]
        x_ok = per_layer("x_ok")
        z_done = [sem(f"z_done{n}") for n in range(HOPS + 1)]
        z_hi_ok = [sem(f"z_hi_ok{n}") for n in range(HOPS)]
        z_ok = [sem(f"z_ok{n}") for n in range(HOPS)]
        h1_hi_ok = sem("h1_hi_ok")
        hh_low_full, hh_low_hi = sem("hh_low_full"), sem("hh_low_hi")
        pair_done, hh_done, s_done = sem("pair_done"), sem("hh_done"), sem("s_done")
        t_min_ok, t_lr_ok, e_min_ok, e_lr_ok = sem("t_min_ok"), sem("t_lr_ok"), sem("e_min_ok"), sem("e_lr_ok")
        e_max_ok, j_max_ok, neg_max_ok = sem("e_max_ok"), sem("j_max_ok"), sem("neg_max_ok")
        w_low_ok, p2_ok, low_sum_ok, all_sum_ok, col_inv_ok = (
            sem(f"{n}_ok") for n in ("w_low", "p2", "low_sum", "all_sum", "col_inv"))
        hh_up_ok, hh_low_ok, out2_done = sem("hh_up_ok"), sem("hh_low_ok"), sem("out2_done")
        bias_ok, hT_diag_ok, h1_done, h1_ok, out3_done = (
            sem(n) for n in ("bias_ok", "hT_diag_ok", "h1_done", "h1_ok", "out3_done"))

        setup = {n: sem(f"setup_{n}") for n in (
            "first_stats", "adjT_hi", "adjT_lo", "low_mask_r", "a_offT_hi", "a_offT_lo",
            "qk_t", "qkT", "m_t", "m_qk", "adj_t", "adjT", "w_hop", "hv_ones",
            "oth_t", "othersT", "u_t", "u_cols", "u_sum", "up1", "low_raw", "any",
            "some", "edgeless", "low_mask",
            "mask3", "cum", "row_tot", "base_t", "row_base", "row_end", "rank", "ended", "sel",
            "g_t", "at_col", "sel_t", "e_cut", "selT", "v_t", "late", "att_a", "att_b", "a_max", "a_neg",
            "a_exp", "a_inv", "a3", "diag_t", "d_t", "diag_row", "a_off", "a_t", "a_offT")}

        x_v = x.rearrange("(g b) (j p) d -> g j p b d", b=GB, p=P)
        out_v = out.rearrange("(g b) (j p) d -> g j p b d", b=GB, p=P)

        block = ctx.enter_context(nc.Block())

        @block.sync
        def _(sp):
            for jt in range(T):
                sp.dma_start(x_all[:, 0, jt * GB:(jt + 1) * GB, :], x_v[0, jt]).then_inc(s_x, 16)
            sp.dma_start(w_raw[:], w_cheb).then_inc(s_w1, 16)
            sp.dma_start(w01[:], w_pair.rearrange("c f g -> f c g")).then_inc(s_l3w, 16)
            sp.dma_start(e_col[:], e_vals.rearrange("a t -> t a")).then_inc(s_l3w, 16)
            sp.dma_start(e_last[:], e_vals[0:1, NE - 1:NE].broadcast_to([P, 1])).then_inc(s_l3w, 16)
            sp.dma_start(bias_b[:], bias.rearrange("(a d) -> a d", a=1).broadcast_to([P, D])).then_inc(s_l3w, 16)
            sp.dma_start(others[:], w_others).then_inc(s_l2w, 16)
            sp.dma_start(w_selfs[:], w_self).then_inc(s_l2w, 16)
            sp.dma_start(att_cols[:], w_att.rearrange("(c p) a -> p (c a)", p=P),
                         allow_slow_non_contiguous=True).then_inc(s_l2w, 16)
            with sp.Fori(1, NG) as g:
                sp.wait_ge(s_x, g * 32)
                for jt in range(T):
                    sp.dma_start(x_all[:, g, jt * GB:(jt + 1) * GB, :], x_v[g, jt]).then_inc(s_x, 16)
            with sp.Fori(0, NG) as g:
                sp.wait_ge(x_ok[3], g + 1)
                for jt in range(T):
                    sp.dma_start(out_v[g, jt], x_all[:, g, jt * GB:(jt + 1) * GB, :]).then_inc(s_out, 16)
            sp.wait_ge(s_out, NG * T * 16)

        @block.gpsimd
        def _(pool):
            nc.gpsimd.memset(ident[:], 0.0).then_inc(s_ident, 1)
            nc.gpsimd.memset(minus_half[:], -0.5).then_inc(s_half, 1)
            nc.gpsimd.memset(eps_t[:], EPS).then_inc(s_half, 1)
            pool.wait_ge(s_ident, 1)
            nc.gpsimd.affine_select(out=ident[:], in_=ident[:], compare_op=ALU.not_equal, fill=1.0,
                                    base=0, pattern=[[-1, P]], channel_multiplier=1).then_inc(s_ident, 1)
            nc.gpsimd.memset(hv1[:, :, D:D + 1], 1.0).then_inc(setup["hv_ones"], 1)

            def inv_std(n, g):
                pool.wait_ge(meanvar_ok[n], g + 1)
                nc.gpsimd.tensor_tensor(var_eps[n][:], meanvar[n][:, :, 1], eps_t[:], ALU.add).then_inc(var_eps_ok[n], 1)
                pool.wait_ge(var_eps_ok[n], g + 1)
                nc.gpsimd.tensor_tensor(rstd[n][:], var_eps[n][:], minus_half[:], ALU.pow).then_inc(rstd_ok[n], 1)

            pool.wait_ge(s_half, 2)
            inv_std(0, 0)
            pool.wait_ge(s_w1, 16)
            nc.gpsimd.tensor_copy(w_hop[:, 0, :], w_raw[:, :, 0])
            for n in range(1, HOPS + 1):
                last = nc.gpsimd.tensor_tensor(w_hop[:, n, :], w_raw[:, :, n], w_raw[:, :, n + HOPS], ALU.add)
            last.then_inc(setup["w_hop"], 1)
            nc.gpsimd.memset(ones[:], 1.0).then_inc(s_consts, 1)
            pool.wait_ge(s_consts, 1)
            nc.gpsimd.affine_select(out=before[:], in_=ones[:], compare_op=ALU.is_gt, fill=0.0, base=0,
                                    pattern=[[1, P]], channel_multiplier=-1)
            nc.gpsimd.iota(t_row[:], pattern=[[1, P]], base=0, channel_multiplier=0,
                           allow_small_or_imprecise_dtypes=True)
            nc.gpsimd.iota(t_one[:], pattern=[[0, 1]], base=1, channel_multiplier=1,
                           allow_small_or_imprecise_dtypes=True).then_inc(s_consts, 1)
            pool.wait_ge(s_l3w, 4 * 16)
            nc.gpsimd.affine_select(out=e_cut[:], in_=e_col[:], compare_op=ALU.not_equal, fill=0.0,
                                    base=-(NE - 1), pattern=[[0, 1]],
                                    channel_multiplier=1).then_inc(setup["e_cut"], 1)
            def off_diagonal():
                pool.wait_ge(setup["a3"], 1)
                for it in range(T):
                    nc.gpsimd.affine_select(out=a_off[:, it, :], in_=a3[:, it, :], compare_op=ALU.not_equal, fill=0.0,
                                            base=it * P, pattern=[[-1, N]],
                                            channel_multiplier=1).then_inc(setup["a_off"], 1)

            def masked(b, g):
                pool.wait_ge(exp_ok[b], g + 1)
                nc.gpsimd.tensor_tensor(pT[:, b], exp_s[:, b], adjT[:], ALU.mult).then_inc(pT_ok[b], 1)

            def diagonal_part(g):
                pool.wait_ge(hT_ok[3], g + 1)
                nc.gpsimd.tensor_tensor(hT_diag[:].rearrange("p (i b) d -> p i b d", b=GB),
                                        hT[3][:].rearrange("p (i b) d -> p i b d", b=GB),
                                        diag_row[:].unsqueeze(2).broadcast_to([P, T, GB, P]),
                                        ALU.mult).then_inc(hT_diag_ok, 1)

            def add_bias(g):
                nc.gpsimd.tensor_tensor(x_all[:, g], x_all[:, g], bias_b[:].unsqueeze(1).broadcast_to([P, TG, D]),
                                        ALU.add).then_inc(bias_ok, 1)

            def pair_low(g):
                pool.wait_ge(hh_up_ok, g + 1)
                nc.gpsimd.tensor_tensor(hh_low[:], hh_up[:], w_low[:].unsqueeze(2).broadcast_to([P, TG, D]),
                                        ALU.mult).then_inc(hh_low_full, 1)
                pool.wait_ge(hh_low_hi, g + 1)
                nc.gpsimd.tensor_tensor(hh_low2[1][:], hh_low[:], hh_low2[0][:].bitcast(fp32),
                                        ALU.subtract).then_inc(hh_low_ok, 1)

            def body(s, layer3=True, next_group=True):
                inv_std(2, s - 2)
                if next_group:
                    inv_std(0, s + 1)
                masked(0, s)
                if layer3:
                    diagonal_part(s - 3)
                    add_bias(s - 3)
                masked(1, s)
                pair_low(s - 2)
                inv_std(1, s)
                inv_std(3, s - 2)

            inv_std(0, 1)
            pool.wait_ge(setup["adjT"], 1)
            masked(0, 0)
            masked(1, 0)
            inv_std(1, 0)
            inv_std(0, 2)
            masked(0, 1)
            off_diagonal()
            masked(1, 1)
            inv_std(1, 1)
            body(2, layer3=False)
            pool.wait_ge(setup["diag_row"], 1)
            with pool.Fori(LAYERS - 1, NG - 1) as s:
                body(s)
            body(NG - 1, next_group=False)
            inv_std(2, NG - 2)
            diagonal_part(NG - 3)
            add_bias(NG - 3)
            pair_low(NG - 2)
            inv_std(2, NG - 1)
            inv_std(3, NG - 2)
            pair_low(NG - 1)
            diagonal_part(NG - 2)
            add_bias(NG - 2)
            inv_std(3, NG - 1)
            diagonal_part(NG - 1)
            add_bias(NG - 1)

        @block.scalar
        def _(act):
            act.dma_start(q_nat[:], q).then_inc(s_qk, 16)
            act.dma_start(k_nat[:], k).then_inc(s_qk, 16)
            act.dma_start(adj_nat[:], adj.rearrange("(t p) j -> p t j", p=P)).then_inc(s_adj, 16)
            act.dma_start(v_sb[:], v).then_inc(s_v, 16)

            def copy(out_ap, in_ap):
                return nc.scalar.activation(out_ap, in_ap, ACT.Copy)

            act.wait_ge(setup["qk_t"], 1)
            copy(qkT[:], tiles(bank[1][0][:, 0:2 * D], 2)).then_inc(setup["qkT"], 1)
            act.wait_ge(setup["m_t"], 1)
            copy(m_qk[:], bank[1][1][:, 0:D]).then_inc(setup["m_qk"], 1)

            def relu_t(n, g):
                act.wait_ge(t_done[n], g + 1)
                nc.scalar.activation(hT[n][:], tiles(bank[n][1 if n == 1 else 0][:]), ACT.Relu).then_inc(hT_ok[n], 1)

            def setup_exp():
                act.wait_ge(setup["a_neg"], 1)
                for it in range(T):
                    nc.scalar.activation(a_exp[:, it, :], att_b[:, it, :], ACT.Exp, bias=a_neg[:, it:it + 1],
                                         accum_out=a_sum[:, it:it + 1]).then_inc(setup["a_exp"], 1)

            def scores(b, g):
                act.wait_ge(score_done[b], g + 1)
                nc.scalar.activation(tanh_s[:, b], tiles(bank[0][1 - b][:], T), ACT.Tanh,
                                     scale=SCORE_SCALE).then_inc(tanh_ok[b], 1)
                act.wait_ge(tanh_ok[b], g + 1)
                nc.scalar.activation(exp_s[:, b], tanh_s[:, b], ACT.Exp, scale=8.0).then_inc(exp_ok[b], 1)

            def high_part(n, g, src):
                act.wait_ge(z_done[n + 1], g + 1)
                copy(z2[n][0][:], tiles(src[:])).then_inc(z_hi_ok[n], 1)

            def copy_g(g):
                act.wait_ge(g_done, g + 1)
                copy(gT[:], tiles(bank[0][1][:])).then_inc(gT_ok, 1)

            def copy_hv(g):
                act.wait_ge(hv_done, g + 1)
                copy(hv1[:, :, 0:D], tiles(bank[0][0][:])).then_inc(hv_ok, 1)

            def pair_exps(g):
                act.wait_ge(neg_max_ok, g + 1)
                nc.scalar.activation(w_low[:], t_diff[:], ACT.Exp).then_inc(w_low_ok, 1)
                for t in range(TG):
                    last = nc.scalar.activation(p2[:, t, :], e_lr[:, t, :], ACT.Exp, bias=neg_max[:, t:t + 1],
                                                accum_out=up_sum[:, t:t + 1])
                last.then_inc(p2_ok, 1)

            def h1_high(g):
                act.wait_ge(h1_done, g + 1)
                copy(h12[0][:], tiles(bank[3][1][:])).then_inc(h1_hi_ok, 1)

            def pair_low_high(g):
                act.wait_ge(hh_low_full, g + 1)
                copy(hh_low2[0][:], hh_low[:]).then_inc(hh_low_hi, 1)

            def body(s, layer3=True, next_group=True):
                high_part(2, s - 1, bank[1][1])
                copy_g(s)
                copy_hv(s)
                scores(0, s)
                high_part(1, s - 1, bank[1][0])
                relu_t(2, s - 2)
                if layer3:
                    relu_t(3, s - 3)
                scores(1, s)
                pair_exps(s - 2)
                high_part(0, s - 1, bank[1][1])
                if layer3:
                    h1_high(s - 3)
                pair_low_high(s - 2)
                relu_t(1, s)
                if next_group:
                    relu_t(0, s + 1)

            relu_t(0, 0)
            copy_g(0)
            copy_hv(0)
            scores(0, 0)
            scores(1, 0)
            act.wait_ge(setup["adjT"], 1)
            copy(adjT2[0][:], adjT[:]).then_inc(setup["adjT_hi"], 1)
            act.wait_ge(setup["low_mask"], 1)
            copy(low_mask_r[:], low_mask[:]).then_inc(setup["low_mask_r"], 1)
            relu_t(0, 1)
            copy_g(1)
            copy_hv(1)
            relu_t(1, 0)
            high_part(2, 0, bank[1][1])
            scores(0, 1)
            setup_exp()
            high_part(1, 0, bank[1][0])
            scores(1, 1)
            high_part(0, 0, bank[1][1])
            relu_t(1, 1)
            relu_t(0, 2)
            act.wait_ge(setup["a_offT"], 1)
            copy(a_offT2[0][:], a_offT[:]).then_inc(setup["a_offT_hi"], 1)
            body(2, layer3=False)
            with act.Fori(LAYERS - 1, NG - 1) as s:
                body(s)
            body(NG - 1, next_group=False)
            high_part(2, NG - 1, bank[1][1])
            relu_t(3, NG - 3)
            high_part(1, NG - 1, bank[1][0])
            h1_high(NG - 3)
            relu_t(2, NG - 2)
            high_part(0, NG - 1, bank[1][1])
            pair_exps(NG - 2)
            pair_low_high(NG - 2)
            relu_t(2, NG - 1)
            pair_exps(NG - 1)
            relu_t(3, NG - 2)
            pair_low_high(NG - 1)
            h1_high(NG - 2)
            relu_t(3, NG - 1)
            h1_high(NG - 1)

        @block.vector
        def _(dve):
            def wait_alone(s, n):
                dve.wait_ge(s_x, 32)
                dve.wait_ge(s, n)

            def moments(n, g, ready, count):
                wait_alone(ready, count)
                for t in range(TG):
                    last = nc.vector.bn_stats(stats[n][:, t, :], x_all[:, g, t, :])
                first = n == 0 and isinstance(g, int) and g == 0
                seen, at = (setup["first_stats"], 1) if first else (stats_seen[n], g if n == 0 else g + 1)
                last.then_inc(seen, 1)
                wait_alone(seen, at)
                for t in range(TG):
                    last = nc.vector.bn_aggr(meanvar[n][:, t, :], stats[n][:, t, :])
                last.then_inc(meanvar_ok[n], 1)

            def normalise(n, g):
                dve.wait_ge(rstd_ok[n], g + 1)
                for t in range(TG):
                    last = nc.vector.tensor_scalar(xn[n][:, t, :], x_all[:, g, t, :], meanvar[n][:, t, 0:1],
                                                   rstd[n][:, t:t + 1], ALU.subtract, ALU.mult)
                last.then_inc(xn_ok[n], 1)

            def adjacency():
                dve.wait_ge(setup["adj_t"], 1)
                nc.vector.tensor_copy(adjT[:], tiles(bank[0][1][:], T)).then_inc(setup["adjT"], 1)

            def adjacency_low():
                dve.wait_ge(setup["adjT_hi"], 1)
                nc.vector.tensor_tensor(adjT2[1][:], adjT[:], adjT2[0][:].bitcast(fp32),
                                        ALU.subtract).then_inc(setup["adjT_lo"], 1)

            def pair_bounds():
                dve.wait_ge(setup["adjT"], 1)
                nc.vector.tensor_scalar(up_bound[:], adjT[:, :, 0:P], 0.0, HUGE, ALU.is_gt,
                                        ALU.mult).then_inc(setup["up1"], 1)
                nc.vector.tensor_scalar(low_mask[:], adjT[:, :, P:N], 0.0, None,
                                        ALU.is_gt).then_inc(setup["low_raw"], 1)
                dve.wait_ge(setup["up1"], 1)
                nc.vector.tensor_reduce(any_up[:], up_bound[:], axis=AX.X, op=ALU.max)
                dve.wait_ge(setup["low_raw"], 1)
                nc.vector.tensor_reduce(any_low[:], low_mask[:], axis=AX.X, op=ALU.max).then_inc(setup["any"], 1)
                dve.wait_ge(setup["any"], 1)
                nc.vector.tensor_tensor(edgeless[:], any_up[:], any_low[:], ALU.max).then_inc(setup["some"], 1)
                nc.vector.tensor_scalar(low_bound[:], any_low[:], HUGE, NEG_PRE, ALU.mult, ALU.add)
                nc.vector.tensor_scalar(up_bound[:], up_bound[:], NEG_PRE, None, ALU.add)
                dve.wait_ge(setup["some"], 1)
                nc.vector.tensor_scalar(edgeless[:], edgeless[:], 0.0, None,
                                        ALU.is_le).then_inc(setup["edgeless"], 1)
                dve.wait_ge(setup["edgeless"], 1)
                for jt in range(T):
                    last = nc.vector.tensor_scalar(low_mask[:, jt, :], low_mask[:, jt, :], edgeless[:, jt:jt + 1],
                                                   None, ALU.max)
                last.then_inc(setup["low_mask"], 1)
                dve.wait_ge(setup["low_mask"], 1)
                nc.vector.tensor_reduce(low_count[:], low_mask[:], axis=AX.X, op=ALU.add)

            def pair_vectors():
                dve.wait_ge(setup["u_t"], 1)
                nc.vector.tensor_copy(u_cols[:], bank[2][1][:, 0:2]).then_inc(setup["u_cols"], 1)
                dve.wait_ge(setup["u_cols"], 1)
                nc.vector.tensor_scalar(u_sum[:], u_cols[:, 0:1].broadcast_to([P, P]), u_cols[:, 1:2], None,
                                        ALU.add).then_inc(setup["u_sum"], 1)

            def edge_counts():
                dve.wait_ge(s_adj, 16)
                nc.vector.tensor_scalar(mask3[:], adj_nat[:], 0.0, None, ALU.is_gt).then_inc(setup["mask3"], 1)
                dve.wait_ge(setup["mask3"], 1)
                for it in range(T):
                    last = nc.vector.tensor_tensor_scan(cum[:, it, :], mask3[:, it, :], mask3[:, it, :], 0.0,
                                                        ALU.add, ALU.max)
                last.then_inc(setup["cum"], 1)
                nc.vector.tensor_scalar(not_edge[:], mask3[:], 1.0, -NEG, ALU.subtract, ALU.mult)
                dve.wait_ge(setup["cum"], 1)
                nc.vector.tensor_copy(row_tot[:], cum[:, :, N - 1]).then_inc(setup["row_tot"], 1)

            def edge_rows():
                dve.wait_ge(setup["base_t"], 1)
                nc.vector.tensor_copy(row_base[:], bank[3][0][:, 0:T]).then_inc(setup["row_base"], 1)
                dve.wait_ge(setup["row_base"], 1)
                nc.vector.tensor_tensor(row_end[:], row_base[:], row_tot[:], ALU.add).then_inc(setup["row_end"], 1)
                for it in range(T):
                    last = nc.vector.scalar_tensor_tensor(rank[:, it, :], cum[:, it, :], row_base[:, it:it + 1],
                                                          mask3[:, it, :], ALU.add, ALU.mult)
                last.then_inc(setup["rank"], 1)
                dve.wait_ge(s_consts, 2)
                dve.wait_ge(setup["row_end"], 1)
                for it in range(T):
                    last = nc.vector.tensor_scalar(ended[:, it, :], t_row[:], row_end[:, it:it + 1], None, ALU.is_lt)
                last.then_inc(setup["ended"], 1)
                dve.wait_ge(setup["ended"], 1)
                for it in range(T):
                    last = nc.vector.scalar_tensor_tensor(sel[:, it, :], t_row[:], row_base[:, it:it + 1],
                                                          ended[:, it, :], ALU.is_ge, ALU.mult)
                last.then_inc(setup["sel"], 1)
                dve.wait_ge(s_l3w, 4 * 16)
                dve.wait_ge(setup["rank"], 1)
                nc.vector.tensor_scalar(late[:], rank[:], float(NE), e_last[:, 0:1], ALU.is_ge,
                                        ALU.mult).then_inc(setup["late"], 1)

            def edge_columns():
                dve.wait_ge(setup["g_t"], 1)
                nc.vector.tensor_scalar(at_col[:], bank[3][0][:, 0:N], t_one[:, 0:1], None,
                                        ALU.is_equal).then_inc(setup["at_col"], 1)
                dve.wait_ge(setup["e_cut"], 1)
                dve.wait_ge(setup["sel_t"], 1)
                nc.vector.tensor_scalar(selT[:], tiles(bank[3][1][:, 0:N], T), e_cut[:, 0:1], None,
                                        ALU.mult).then_inc(setup["selT"], 1)

            def edge_values():
                dve.wait_ge(setup["v_t"], 1)
                dve.wait_ge(setup["late"], 1)
                nc.vector.tensor_tensor(att_a[:], tiles(bank[3][0][:], T), late[:], ALU.add).then_inc(setup["att_a"], 1)
                dve.wait_ge(setup["att_a"], 1)
                nc.vector.tensor_tensor(att_b[:], att_a[:], not_edge[:], ALU.add).then_inc(setup["att_b"], 1)
                dve.wait_ge(setup["att_b"], 1)
                nc.vector.tensor_reduce(a_max[:], att_b[:], axis=AX.X, op=ALU.max).then_inc(setup["a_max"], 1)
                dve.wait_ge(setup["a_max"], 1)
                nc.vector.tensor_scalar(a_neg[:], a_max[:], -1.0, None, ALU.mult).then_inc(setup["a_neg"], 1)

            def edge_softmax():
                dve.wait_ge(setup["a_exp"], T)
                nc.vector.reciprocal(a_inv[:], a_sum[:]).then_inc(setup["a_inv"], 1)
                dve.wait_ge(setup["a_inv"], 1)
                for it in range(T):
                    last = nc.vector.tensor_scalar(a3[:, it, :], a_exp[:, it, :], a_inv[:, it:it + 1], None, ALU.mult)
                last.then_inc(setup["a3"], 1)
                dve.wait_ge(setup["a3"], 1)
                for it in range(T):
                    last = nc.vector.tensor_tensor(diag_t[:, it, :], a3[:, it, it * P:(it + 1) * P], ident[:], ALU.mult)
                last.then_inc(setup["diag_t"], 1)

            def edge_transposed():
                dve.wait_ge(setup["d_t"], 1)
                nc.vector.tensor_copy(diag_row[:], tiles(bank[3][1][:, 0:N], T)).then_inc(setup["diag_row"], 1)
                dve.wait_ge(setup["a_t"], 1)
                nc.vector.tensor_copy(a_offT[:], tiles(bank[3][0][:], T)).then_inc(setup["a_offT"], 1)

            def edge_transposed_low():
                dve.wait_ge(setup["a_offT_hi"], 1)
                nc.vector.tensor_tensor(a_offT2[1][:], a_offT[:], a_offT2[0][:].bitcast(fp32),
                                        ALU.subtract).then_inc(setup["a_offT_lo"], 1)

            def add_to_x(n, g, src):
                nc.vector.tensor_tensor(x_all[:, g], tiles(src[:]), x_all[:, g], ALU.add).then_inc(x_ok[n], 1)

            def pair_scores(g):
                dve.wait_ge(s_done, g + 1)
                nc.vector.tensor_tensor(e_min[:].rearrange("p (j b) i -> p j b i", j=T),
                                        bank[2][1][:].rearrange("p (j b i) -> p j b i", j=T, b=GB),
                                        up_bound[:].unsqueeze(2).broadcast_to([P, T, GB, P]),
                                        ALU.min).then_inc(e_min_ok, 1)
                dve.wait_ge(e_min_ok, g + 1)
                nc.vector.scalar_tensor_tensor(e_lr[:], e_min[:], SLOPE, e_min[:], ALU.mult,
                                               ALU.max).then_inc(e_lr_ok, 1)
                dve.wait_ge(pair_done, g + 1)
                nc.vector.tensor_tensor(t_min[:].rearrange("p (j b) -> p j b", j=T),
                                        bank[3][0][:, 0:GB].unsqueeze(1).broadcast_to([P, T, GB]),
                                        low_bound[:].unsqueeze(2).broadcast_to([P, T, GB]),
                                        ALU.min).then_inc(t_min_ok, 1)
                dve.wait_ge(e_lr_ok, g + 1)
                nc.vector.tensor_reduce(e_max[:], e_lr[:], axis=AX.X, op=ALU.max).then_inc(e_max_ok, 1)
                dve.wait_ge(t_min_ok, g + 1)
                nc.vector.scalar_tensor_tensor(t_lr[:], t_min[:], SLOPE, t_min[:], ALU.mult,
                                               ALU.max).then_inc(t_lr_ok, 1)
                dve.wait_ge(e_max_ok, g + 1)
                dve.wait_ge(t_lr_ok, g + 1)
                nc.vector.tensor_tensor(j_max[:], e_max[:], t_lr[:], ALU.max).then_inc(j_max_ok, 1)
                dve.wait_ge(j_max_ok, g + 1)
                nc.vector.tensor_tensor(t_diff[:], t_lr[:], j_max[:], ALU.subtract)
                nc.vector.tensor_scalar(neg_max[:], j_max[:], -1.0, None, ALU.mult).then_inc(neg_max_ok, 1)

            def pair_sums(g):
                dve.wait_ge(w_low_ok, g + 1)
                nc.vector.tensor_tensor(low_sum[:].rearrange("p (j b) -> p j b", j=T),
                                        w_low[:].rearrange("p (j b) -> p j b", j=T),
                                        low_count[:].unsqueeze(2).broadcast_to([P, T, GB]),
                                        ALU.mult).then_inc(low_sum_ok, 1)
                dve.wait_ge(low_sum_ok, g + 1)
                dve.wait_ge(p2_ok, g + 1)
                nc.vector.tensor_tensor(all_sum[:], low_sum[:], up_sum[:], ALU.add).then_inc(all_sum_ok, 1)
                dve.wait_ge(all_sum_ok, g + 1)
                nc.vector.reciprocal(col_inv[:], all_sum[:]).then_inc(col_inv_ok, 1)
                dve.wait_ge(col_inv_ok, g + 1)
                dve.wait_ge(hh_done, g + 1)
                nc.vector.tensor_tensor(hh_up[:], tiles(bank[2][0][:]),
                                        col_inv[:].unsqueeze(2).broadcast_to([P, TG, D]),
                                        ALU.mult).then_inc(hh_up_ok, 1)

            def low_part(out_pair, src, hi_ok, ok, count):
                dve.wait_ge(hi_ok, count)
                nc.vector.tensor_tensor(out_pair[1][:], tiles(src[:]), out_pair[0][:].bitcast(fp32),
                                        ALU.subtract).then_inc(ok, 1)

            def attention_out(g):
                for b in range(GB):
                    dve.wait_ge(o_done[b], g + 1)
                    o = bank[0][1 - b][:, 0:T * (D + 1)].rearrange("p (i d) -> p i d", i=T)
                    nc.vector.reciprocal(row_inv[:, b, :], o[:, :, D]).then_inc(row_inv_ok[b], 1)
                    dve.wait_ge(row_inv_ok[b], g + 1)
                    for it in range(T):
                        t = it * GB + b
                        last = nc.vector.scalar_tensor_tensor(x_all[:, g, t, :], o[:, it, 0:D],
                                                              row_inv[:, b, it:it + 1], x_all[:, g, t, :],
                                                              ALU.mult, ALU.add)
                last.then_inc(x_ok[0], 1)

            def z_low(n, g, src):
                low_part(z2[n], src, z_hi_ok[n], z_ok[n], g + 1)

            def h1_low(g):
                low_part(h12, bank[3][1], h1_hi_ok, h1_ok, g + 1)

            def layer1_out(g):
                dve.wait_ge(z_done[0], g + 1)
                add_to_x(1, g, bank[1][0])

            def layer2_out(g):
                dve.wait_ge(out2_done, g + 1)
                add_to_x(2, g, bank[2][1])

            def layer3_out(g):
                dve.wait_ge(bias_ok, g + 1)
                dve.wait_ge(out3_done, g + 1)
                add_to_x(3, g, bank[3][1])

            def body(s, layer3=True, next_group=True):
                moments(2, s - 2, x_ok[1], s - 1)
                z_low(2, s - 1, bank[1][1])
                if layer3:
                    normalise(3, s - 3)
                normalise(2, s - 2)
                if next_group:
                    moments(0, s + 1, s_x, s * 32 + 64)
                z_low(1, s - 1, bank[1][0])
                pair_scores(s - 2)
                if next_group:
                    dve.wait_ge(t_done[0], s + 1)
                    normalise(0, s + 1)
                pair_sums(s - 2)
                if layer3:
                    h1_low(s - 3)
                attention_out(s)
                moments(1, s, x_ok[0], s + 1)
                z_low(0, s - 1, bank[1][1])
                if layer3:
                    layer3_out(s - 3)
                normalise(1, s)
                layer2_out(s - 2)
                moments(3, s - 2, x_ok[2], s - 1)
                layer1_out(s - 1)

            moments(0, 0, s_x, 32)
            normalise(0, 0)
            adjacency()
            edge_counts()
            pair_bounds()
            moments(0, 1, s_x, 64)
            edge_rows()
            dve.wait_ge(setup["oth_t"], 1)
            nc.vector.tensor_copy(othersT[:], bank[2][0][:, 0:D]).then_inc(setup["othersT"], 1)
            dve.wait_ge(t_done[0], 1)
            normalise(0, 1)
            edge_columns()
            attention_out(0)
            moments(1, 0, x_ok[0], 1)
            adjacency_low()
            pair_vectors()
            normalise(1, 0)
            edge_values()
            z_low(2, 0, bank[1][1])
            edge_softmax()
            moments(0, 2, s_x, 96)
            z_low(1, 0, bank[1][0])
            dve.wait_ge(t_done[0], 2)
            normalise(0, 2)
            z_low(0, 0, bank[1][1])
            attention_out(1)
            moments(1, 1, x_ok[0], 2)
            layer1_out(0)
            normalise(1, 1)
            edge_transposed()
            body(2, layer3=False)
            edge_transposed_low()
            with dve.Fori(LAYERS - 1, NG - 1) as s:
                body(s)
            body(NG - 1, next_group=False)
            moments(2, NG - 2, x_ok[1], NG - 1)
            z_low(2, NG - 1, bank[1][1])
            normalise(3, NG - 3)
            normalise(2, NG - 2)
            z_low(1, NG - 1, bank[1][0])
            h1_low(NG - 3)
            z_low(0, NG - 1, bank[1][1])
            pair_scores(NG - 2)
            pair_sums(NG - 2)
            layer1_out(NG - 1)
            moments(2, NG - 1, x_ok[1], NG)
            layer3_out(NG - 3)
            normalise(2, NG - 1)
            layer2_out(NG - 2)
            moments(3, NG - 2, x_ok[2], NG - 1)
            pair_scores(NG - 1)
            normalise(3, NG - 2)
            pair_sums(NG - 1)
            h1_low(NG - 2)
            layer2_out(NG - 1)
            moments(3, NG - 1, x_ok[2], NG)
            layer3_out(NG - 2)
            normalise(3, NG - 1)
            h1_low(NG - 1)
            layer3_out(NG - 1)

        @block.tensor
        def _(pe):
            def mm(o, lhsT, rhs, start=True, stop=True, shared=False):
                return nc.tensor.matmul(o, lhsT, rhs, start=start, stop=stop, skip_group_check=shared)

            def transposes(n, g):
                pe.wait_ge(xn_ok[n], g + 1)
                bk = tiles(bank[n][1 if n == 1 else 0][:])
                for t in range(TG):
                    to = t % GB * T + t // GB if n == 2 else t
                    last = nc.tensor.transpose(bk[:, to, :], xn[n][:, t, :], ident[:])
                last.then_inc(t_done[n], 1)

            def bank_read(s, n):
                if not isinstance(n, int) or n > 0:
                    pe.wait_ge(s, n)

            def mm_split(o, lhsT2, rhs2, start, stop):
                pairs = [(0, 0), (0, 1), (1, 0)][:3 if len(lhsT2) == 2 else 2]
                for n, (c, d) in enumerate(pairs):
                    last = mm(o, lhsT2[c], rhs2[d], start=start and n == 0, stop=stop and n == len(pairs) - 1,
                              shared=True)
                return last

            def horner_w(bk, hop):
                for t in range(TG):
                    last = mm(tiles(bk[:])[:, t, :], hT[1][:, t, :], w_hop[:, hop, :], start=t == 0,
                              stop=hop == HOPS, shared=True)
                return last

            def horner_adj(bk, prev2, it):
                o = tiles(bk[:])[:, it * GB:(it + 1) * GB, :]
                for jt in range(T):
                    last = mm_split(o, [a[:, jt, it * P:(it + 1) * P] for a in adjT2],
                                    [p[:, jt * GB:(jt + 1) * GB, :] for p in prev2], False, jt == T - 1)
                return last

            def scores(b, g):
                gv = gT[:].rearrange("p (i b) d -> p i b d", b=GB)
                for jt in range(T):
                    last = mm(tiles(bank[0][1 - b][:], T)[:, jt, :].rearrange("p (i d) -> p i d", i=T),
                              hT[0][:, jt * GB + b, :], gv[:, :, b, :])
                last.then_inc(score_done[b], 1)

            def project(g):
                pe.wait_ge(hT_ok[0], g + 1)
                mm(bank[0][1][:], m_qk[:], hT[0][:].rearrange("p t d -> p (t d)")).then_inc(g_done, 1)
                for t in range(TG):
                    last = mm(tiles(bank[0][0][:])[:, t, :], hT[0][:, t, :], v_sb[:])
                last.then_inc(hv_done, 1)

            def scores_0(g):
                pe.wait_ge(gT_ok, g + 1)
                scores(0, g)

            def scores_1(g):
                pe.wait_ge(hv_ok, g + 1)
                scores(1, g)

            def attend(g):
                for b in range(GB):
                    pe.wait_ge(pT_ok[b], g + 1)
                    o = bank[0][1 - b][:, 0:T * (D + 1)].rearrange("p (i d) -> p i d", i=T)
                    for it in range(T):
                        for jt in range(T):
                            last = mm(o[:, it, :], pT[:, b, jt, it * P:(it + 1) * P], hv1[:, jt * GB + b, :],
                                      start=jt == 0, stop=jt == T - 1)
                    last.then_inc(o_done[b], 1)

            def horner_3(g):
                pe.wait_ge(hT_ok[1], g + 1)
                horner_w(bank[1][1], HOPS).then_inc(z_done[HOPS], 1)

            def horner_2(g):
                bank_read(x_ok[1], g)
                horner_w(bank[1][0], 2)
                pe.wait_ge(z_ok[2], g + 1)
                horner_adj(bank[1][0], z2[2], 0)
                horner_adj(bank[1][0], z2[2], 1).then_inc(z_done[2], 1)

            def horner_1(g):
                horner_w(bank[1][1], 1)
                pe.wait_ge(z_ok[1], g + 1)
                horner_adj(bank[1][1], z2[1], 0)
                horner_adj(bank[1][1], z2[1], 1).then_inc(z_done[1], 1)

            def horner_0_first(g):
                horner_w(bank[1][0], 0)
                pe.wait_ge(z_ok[0], g + 1)
                horner_adj(bank[1][0], z2[0], 0)

            def horner_0_second(g):
                horner_adj(bank[1][0], z2[0], 1).then_inc(z_done[0], 1)

            def pair_products(g, relus):
                pe.wait_ge(hT_ok[2], g + 1)
                bank_read(x_ok[2], g)
                pairs = hT[2][:].rearrange("p (b i) (c r) -> p r b (i c)", b=GB, r=2)
                mm(bank[2][1][:].rearrange("p (j b i) -> p j b i", j=T, b=GB), u_sum[:], pairs).then_inc(s_done, 1)
                bank_read(hT_ok[3], relus)
                for b in range(GB):
                    for r in range(2):
                        last = mm(bank[3][0][:, b:b + 1], pairs[:, r, b, :], u_cols[:, r:r + 1],
                                  start=r == 0, stop=r == 1)
                last.then_inc(pair_done, 1)
                for t in range(TG):
                    last = mm(tiles(bank[2][0][:])[:, t, :], hT[2][:, t % GB * T + t // GB, :], others[:])
                last.then_inc(hh_done, 1)

            def pair_upper(g):
                o = tiles(bank[2][1][:])
                pe.wait_ge(p2_ok, g + 1)
                pe.wait_ge(e_min_ok, g + 1)
                pe.wait_ge(hh_up_ok, g + 1)
                for b in range(GB):
                    mm(o[:, b, :], hT[2][:, b * T, :], w_selfs[:], stop=False)
                    for jt in range(T):
                        mm(o[:, b, :], p2[:, jt * GB + b, :], hh_up[:, jt * GB + b, :], start=False,
                           stop=jt == T - 1)
                for b in range(GB):
                    mm(o[:, GB + b, :], hT[2][:, b * T + 1, :], w_selfs[:], start=b == 0, stop=False, shared=True)

            def pair_lower(g):
                o = tiles(bank[2][1][:])
                pe.wait_ge(hh_low_ok, g + 1)
                for jt in range(T):
                    last = mm_split(o[:, GB:2 * GB, :], [low_mask_r[:, jt, :]],
                                    [p[:, jt * GB:(jt + 1) * GB, :] for p in hh_low2], False, jt == T - 1)
                last.then_inc(out2_done, 1)

            def learnt_h(g):
                pe.wait_ge(hT_ok[3], g + 1)
                bank_read(x_ok[3], g)
                for t in range(TG):
                    last = mm(tiles(bank[3][1][:])[:, t, :], hT[3][:, t, :], w01[:, 1, :])
                last.then_inc(h1_done, 1)

            def learnt_out(g):
                o = tiles(bank[3][1][:])
                pe.wait_ge(hT_diag_ok, g + 1)
                pe.wait_ge(h1_ok, g + 1)
                for t in range(TG):
                    mm(o[:, t, :], hT_diag[:, t, :], w01[:, 0, :], start=t == 0, stop=False, shared=True)
                for it in range(T):
                    for jt in range(T):
                        last = mm_split(o[:, it * GB:(it + 1) * GB, :],
                                        [a[:, jt, it * P:(it + 1) * P] for a in a_offT2],
                                        [p[:, jt * GB:(jt + 1) * GB, :] for p in h12], False, jt == T - 1)
                last.then_inc(out3_done, 1)

            def transposes_3(g, pairs):
                pe.wait_ge(t_min_ok, pairs)
                transposes(3, g)

            def body(s, layer3=True, next_group=True):
                horner_3(s - 1)
                project(s)
                scores_0(s)
                horner_2(s - 1)
                transposes(2, s - 2)
                if layer3:
                    transposes_3(s - 3, s - 2)
                scores_1(s)
                pair_products(s - 2, s - 2)
                horner_1(s - 1)
                if layer3:
                    learnt_h(s - 3)
                attend(s)
                pair_upper(s - 2)
                if layer3:
                    learnt_out(s - 3)
                pair_lower(s - 2)
                horner_0_first(s - 1)
                transposes(1, s)
                horner_0_second(s - 1)
                if next_group:
                    pe.wait_ge(x_ok[0], s + 1)
                    transposes(0, s + 1)

            pe.wait_ge(s_ident, 2)
            pe.wait_ge(s_qk, 32)
            bk = tiles(bank[1][0][:, 0:2 * D], 2)
            nc.tensor.transpose(bk[:, 0, :], q_nat[:], ident[:])
            nc.tensor.transpose(bk[:, 1, :], k_nat[:], ident[:]).then_inc(setup["qk_t"], 1)
            pe.wait_ge(s_adj, 16)
            bk = tiles(bank[0][1][:], T)
            for it in range(T):
                for jt in range(T):
                    last = nc.tensor.transpose(bk[:, jt, it * P:(it + 1) * P], adj_nat[:, it, jt * P:(jt + 1) * P],
                                               ident[:])
            last.then_inc(setup["adj_t"], 1)
            pe.wait_ge(setup["qkT"], 1)
            mm(bank[1][1][:, 0:D], qkT[:, 0, :], qkT[:, 1, :]).then_inc(setup["m_t"], 1)
            transposes(0, 0)
            for n in ("adjT", "m_qk", "hv_ones"):
                pe.wait_ge(setup[n], 1)
            pe.wait_ge(s_v, 16)
            project(0)
            pe.wait_ge(setup["row_tot"], 1)
            pe.wait_ge(s_consts, 2)
            mm(bank[3][0][:, 0:1], before[:], row_tot[:, 0:1])
            mm(bank[3][0][:, 1:2], ones[:], row_tot[:, 0:1], stop=False)
            mm(bank[3][0][:, 1:2], before[:], row_tot[:, 1:2], start=False).then_inc(setup["base_t"], 1)
            scores_0(0)
            scores_1(0)
            pe.wait_ge(s_l2w, 48)
            nc.tensor.transpose(bank[2][0][:, 0:D], others[:], ident[:]).then_inc(setup["oth_t"], 1)
            pe.wait_ge(setup["sel"], 1)
            pe.wait_ge(setup["rank"], 1)
            pe.wait_ge(setup["row_base"], 1)
            for it in range(T):
                last = mm(bank[3][0][:, 0:N], sel[:, it, :], rank[:, it, :], start=it == 0, stop=it == T - 1)
            last.then_inc(setup["g_t"], 1)
            for it in range(T):
                last = nc.tensor.transpose(bank[3][1][:, it * P:(it + 1) * P], sel[:, it, :], ident[:])
            last.then_inc(setup["sel_t"], 1)
            attend(0)
            pe.wait_ge(setup["othersT"], 1)
            mm(bank[2][1][:, 0:2], othersT[:], att_cols[:]).then_inc(setup["u_t"], 1)
            pe.wait_ge(setup["at_col"], 1)
            pe.wait_ge(setup["selT"], 1)
            for it in range(T):
                last = mm(bank[3][0][:, it * N:(it + 1) * N], selT[:, it, :], at_col[:])
            last.then_inc(setup["v_t"], 1)
            pe.wait_ge(x_ok[0], 1)
            transposes(0, 1)
            project(1)
            transposes(1, 0)
            for n in ("w_hop", "adjT_hi", "adjT_lo"):
                pe.wait_ge(setup[n], 1)
            horner_3(0)
            scores_0(1)
            horner_2(0)
            scores_1(1)
            horner_1(0)
            attend(1)
            pe.wait_ge(setup["a_off"], T)
            pe.wait_ge(setup["att_a"], 1)
            bk = tiles(bank[3][0][:], T)
            for it in range(T):
                for jt in range(T):
                    last = nc.tensor.transpose(bk[:, jt, it * P:(it + 1) * P], a_off[:, it, jt * P:(jt + 1) * P],
                                               ident[:])
            last.then_inc(setup["a_t"], 1)
            pe.wait_ge(setup["diag_t"], 1)
            for it in range(T):
                last = mm(bank[3][1][:, it * P:(it + 1) * P], ones[:], diag_t[:, it, :])
            last.then_inc(setup["d_t"], 1)
            horner_0_first(0)
            horner_0_second(0)
            pe.wait_ge(x_ok[0], 2)
            transposes(0, 2)
            transposes(1, 1)
            pe.wait_ge(setup["u_sum"], 1)
            pe.wait_ge(setup["a_offT"], 1)
            pe.wait_ge(setup["low_mask_r"], 1)
            body(2, layer3=False)
            for n in ("diag_row", "a_offT_hi", "a_offT_lo"):
                pe.wait_ge(setup[n], 1)
            with pe.Fori(LAYERS - 1, NG - 1) as s:
                body(s)
            body(NG - 1, next_group=False)
            horner_3(NG - 1)
            transposes_3(NG - 3, NG - 2)
            horner_2(NG - 1)
            learnt_h(NG - 3)
            transposes(2, NG - 2)
            horner_1(NG - 1)
            pair_products(NG - 2, NG - 2)
            horner_0_first(NG - 1)
            horner_0_second(NG - 1)
            learnt_out(NG - 3)
            pair_upper(NG - 2)
            pair_lower(NG - 2)
            transposes(2, NG - 1)
            pair_products(NG - 1, NG - 2)
            transposes_3(NG - 2, NG)
            learnt_h(NG - 2)
            pair_upper(NG - 1)
            pair_lower(NG - 1)
            learnt_out(NG - 2)
            transposes_3(NG - 1, NG)
            learnt_h(NG - 1)
            learnt_out(NG - 1)


_INS = ['x', 'adj', 'L0_gnn_q', 'L0_gnn_k', 'L0_gnn_v', 'L1_gnn_weight_1', 'L2_gnn_others_weight',
        'L2_gnn_self_weight', 'L2_gnn_att_weight', 'L3_gnn_W', 'L3_gnn_e', 'L3_gnn_bias']


def kernel(**inputs):
    import numpy as _np
    import concourse.bacc as _bacc
    from concourse import mybir as _mybir
    from concourse.bass_utils import run_bass_kernel_spmd as _run

    nc = _bacc.Bacc("TRN2", target_bir_lowering=False, num_devices=1)
    arrays, args = {}, []
    for name in _INS:
        a = _np.ascontiguousarray(inputs[name])
        arrays[f"in_{name}_dram"] = a
        args.append(nc.dram_tensor(f"in_{name}_dram", a.shape, _mybir.dt.from_np(a.dtype), kind="ExternalInput").ap())
    out = nc.dram_tensor("out_dram", inputs["x"].shape, _mybir.dt.float32, kind="ExternalOutput").ap()
    four_layer_gnn(nc, *args, out)
    r = _run(nc, [arrays], core_ids=[0])
    return r.results[0]["out_dram"]
```

```python
import math
from contextlib import ExitStack

import concourse.bass as bass
from concourse import mybir


def four_layer_gnn(nc, x, adj, q, k, v, w_cheb, w_others, w_self, w_att, w_pair, e_vals, bias, out):
    fp32 = mybir.dt.float32
    f32r = mybir.dt.float32r
    ALU = mybir.AluOpType
    ACT = mybir.ActivationFunctionType
    AX = mybir.AxisListType

    P = 128
    B, N, D = x.shape
    assert D == P and N == 2 * P
    T = N // P
    GB = 2
    NG = B // GB
    TG = T * GB
    CH = TG * D
    LAYERS = 4
    SCORE_SCALE = 1.0 / (8.0 * math.sqrt(D))
    EPS = 1e-5
    SLOPE = 0.1
    NEG = -9.0e15
    NEG_PRE = NEG / SLOPE
    HUGE = 3.0e38
    KW = w_cheb.shape[2]
    HOPS = (KW - 1) // 2
    NE = e_vals.shape[1]
    assert NE == P and NG > LAYERS

    ctx = ExitStack()
    with ctx:
        def sb(name, shape, dt=fp32):
            return ctx.enter_context(nc.sbuf_tensor(name, shape, dt))

        def halves(name, shape):
            return [sb(f"{name}_{n}", shape, f32r) for n in ("hi", "lo")]

        def sem(name):
            return ctx.enter_context(nc.semaphore(name))

        def per_layer(name, layers=range(LAYERS)):
            return {n: sem(f"{name}{n}") for n in layers}

        x_all = sb("x_all", [P, NG, TG, D])
        xn = [sb(f"xn{n}", [P, TG, D]) for n in range(LAYERS)]
        hT = {n: sb(f"hT{n}", [P, TG, P]) for n in (0, 2)}
        hT2 = {n: halves(f"hT{n}", [P, TG, P]) for n in (1, 3)}
        stats = [sb(f"stats{n}", [P, TG, 6]) for n in range(LAYERS)]
        meanvar = [sb(f"meanvar{n}", [P, TG, 2]) for n in range(LAYERS)]
        var_eps = [sb(f"var_eps{n}", [P, TG]) for n in range(LAYERS)]
        rstd = [sb(f"rstd{n}", [P, TG]) for n in range(LAYERS)]
        minus_half, minus_one, eps_t = (sb(n, [P, TG]) for n in ("minus_half", "minus_one", "eps_t"))
        minus_mean = sb("minus_mean", [P, TG])
        shift = sb("shift", [P, TG])

        ident = sb("ident", [P, P])
        adj_nat = sb("adj_nat", [P, T, N])
        adjT = sb("adjT", [P, T, N])

        q_nat, k_nat, v_sb = sb("q_nat", [P, D]), sb("k_nat", [P, D]), sb("v_sb", [P, D])
        qkT = sb("qkT", [P, 2, D])
        m_qk = sb("m_qk", [P, D])
        gT = sb("gT", [P, TG, P])
        hv1 = sb("hv1", [P, TG, D + 1])
        tanh_s = sb("tanh_s", [P, GB, T, N])
        exp_s = sb("exp_s", [P, GB, T, N])
        pT = sb("pT", [P, GB, T, N])
        row_inv = sb("row_inv", [P, GB, T])

        w_raw = sb("w_raw", [P, D, KW])
        w_hop = sb("w_hop", [P, HOPS + 1, D])
        w_hop2 = halves("w_hop", [P, HOPS + 1, D])
        adjT2 = halves("adjT", [P, T, N])
        z2 = [halves(f"z{n}", [P, TG, D]) for n in range(HOPS)]

        others = sb("others", [P, D])
        w_selfs = sb("w_selfs", [P, D])
        att_cols = sb("att_cols", [P, 2])
        othersT = sb("othersT", [P, D])
        u_cols = sb("u_cols", [P, 2])
        u_sum = sb("u_sum", [P, P])
        up_bound = sb("up_bound", [P, T, P])
        low_mask = sb("low_mask", [P, T, P])
        any_up, any_low, edgeless = sb("any_up", [P, T]), sb("any_low", [P, T]), sb("edgeless", [P, T])
        low_count, low_bound = sb("low_count", [P, T]), sb("low_bound", [P, T])
        e_min = sb("e_min", [P, TG, P])
        e_lr = sb("e_lr", [P, TG, P])
        p2 = sb("p2", [P, TG, P])
        t_min, t_lr = sb("t_min", [P, TG]), sb("t_lr", [P, TG])
        e_max, j_max, neg_max = sb("e_max", [P, TG]), sb("j_max", [P, TG]), sb("neg_max", [P, TG])
        t_diff, w_low, low_sum = sb("t_diff", [P, TG]), sb("w_low", [P, TG]), sb("low_sum", [P, TG])
        up_sum, all_sum, col_inv = sb("up_sum", [P, TG]), sb("all_sum", [P, TG]), sb("col_inv", [P, TG])
        hh_up, hh_low = sb("hh_up", [P, TG, D]), sb("hh_low", [P, TG, D])
        low_mask_r = sb("low_mask_r", [P, T, P], f32r)
        hh_low2 = halves("hh_low", [P, TG, D])

        w10 = sb("w10", [P, 2, D])
        w102 = halves("w10", [P, 2, D])
        e_col, e_cut, e_last = sb("e_col", [P, 1]), sb("e_cut", [P, 1]), sb("e_last", [P, 1])
        bias_b = sb("bias_b", [P, D])
        mask3, cum = sb("mask3", [P, T, N]), sb("cum", [P, T, N])
        rank = sb("rank", [P, T, N])
        row_tot, row_base, row_end = sb("row_tot", [P, T]), sb("row_base", [P, T]), sb("row_end", [P, T])
        before, ones = sb("before", [P, P]), sb("ones", [P, P])
        t_row, t_one = sb("t_row", [P, P]), sb("t_one", [P, 1])
        ended, sel = sb("ended", [P, T, P]), sb("sel", [P, T, P])
        at_col, selT = sb("at_col", [P, N]), sb("selT", [P, T, P])
        late, not_edge = sb("late", [P, T, N]), sb("not_edge", [P, T, N])
        att_a, att_b = sb("att_a", [P, T, N]), sb("att_b", [P, T, N])
        a_max, a_neg, a_sum, a_inv = (sb(f"a_{n}", [P, T]) for n in ("max", "neg", "sum", "inv"))
        a_exp, a3 = sb("a_exp", [P, T, N]), sb("a3", [P, T, N])
        diag_t = sb("diag_t", [P, T, P])
        a_off = sb("a_off", [P, T, N])
        a_offT = sb("a_offT", [P, T, N])
        a_offT2 = halves("a_offT", [P, T, N])
        h12 = halves("h1", [P, TG, D])
        diag = sb("diag", [P, T])
        h0_diag = sb("h0_diag", [P, TG, D])
        h0_bias = sb("h0_bias", [P, TG, D])

        bank = {n: [ctx.enter_context(nc.psum_tensor(f"bank{n}{c}", [P, CH], fp32)) for c in "ab"]
                for n in (0, 2)}
        wide = {n: ctx.enter_context(nc.psum_tensor(f"wide{n}", [P, T, 2, GB * D], fp32)) for n in (1, 3)}
        for n in wide:
            bank[n] = [wide[n][:, it].rearrange("p c d -> p (c d)") for it in range(T)]
        assert T == 2

        def by_it(ap):
            return ap.rearrange("p (i b) d -> p i (b d)", i=T)

        def tiles(ap, n=TG):
            return ap.rearrange("p (t d) -> p t d", t=n)

        s_x, s_out = sem("x_loaded"), sem("out_stored")
        s_adj, s_qk, s_v, s_w1, s_l2w, s_l3w = (sem(f"loaded_{n}") for n in ("adj", "qk", "v", "w1", "l2", "l3"))
        s_half, s_ident = sem("minus_half_set"), sem("ident_set")
        s_consts = sem("consts_set")
        stats_seen = per_layer("stats_seen")
        meanvar_ok = per_layer("meanvar_ok")
        var_eps_ok = per_layer("var_eps_ok")
        rstd_ok = per_layer("rstd_ok")
        shift_ok = sem("shift_ok")
        xn_ok = per_layer("xn_ok")
        t_done = per_layer("t_done")
        hT_ok = per_layer("hT_ok")
        hT_low_ok = {n: sem(f"hT_low_ok{n}") for n in (1, 3)}

        g_done, hv_done = sem("g_done"), sem("hv_done")
        gT_ok, hv_ok = sem("gT_ok"), sem("hv_ok")
        score_done = [sem(f"score_done{b}") for b in range(GB)]
        tanh_ok = [sem(f"tanh_ok{b}") for b in range(GB)]
        exp_ok = [sem(f"exp_ok{b}") for b in range(GB)]
        pT_ok = [sem(f"pT_ok{b}") for b in range(GB)]
        o_done = [sem(f"o_done{b}") for b in range(GB)]
        row_inv_ok = [sem(f"row_inv_ok{b}") for b in range(GB)]
        x_ok = per_layer("x_ok")
        z_done = [sem(f"z_done{n}") for n in range(HOPS + 1)]
        z_hi_ok = [sem(f"z_hi_ok{n}") for n in range(HOPS)]
        z_ok = [sem(f"z_ok{n}") for n in range(HOPS)]
        h1_hi_ok = sem("h1_hi_ok")
        hh_low_full, hh_low_hi = sem("hh_low_full"), sem("hh_low_hi")
        pair_done, hh_done, s_done = sem("pair_done"), sem("hh_done"), sem("s_done")
        t_min_ok, t_lr_ok, e_min_ok, e_lr_ok = sem("t_min_ok"), sem("t_lr_ok"), sem("e_min_ok"), sem("e_lr_ok")
        e_max_ok, j_max_ok, neg_max_ok = sem("e_max_ok"), sem("j_max_ok"), sem("neg_max_ok")
        w_low_ok, p2_ok, low_sum_ok, all_sum_ok, col_inv_ok = (
            sem(f"{n}_ok") for n in ("w_low", "p2", "low_sum", "all_sum", "col_inv"))
        hh_up_ok, hh_low_ok, out2_done = sem("hh_up_ok"), sem("hh_low_ok"), sem("out2_done")
        h0_bias_ok, bias_ok, h0_diag_ok, h1_done, h1_ok, out3_done = (
            sem(n) for n in ("h0_bias_ok", "bias_ok", "h0_diag_ok", "h1_done", "h1_ok", "out3_done"))

        setup = {n: sem(f"setup_{n}") for n in (
            "first_stats", "adjT_hi", "adjT_lo", "low_mask_r", "a_offT_hi", "a_offT_lo",
            "qk_t", "qkT", "m_t", "m_qk", "adj_t", "adjT", "w_hop", "w_hop_hi", "w_hop_lo", "w10_hi", "w10_lo", "hv_ones",
            "oth_t", "othersT", "u_t", "u_cols", "u_sum", "up1", "low_raw", "any",
            "some", "edgeless", "low_mask",
            "mask3", "cum", "row_tot", "base_t", "row_base", "row_end", "rank", "ended", "sel",
            "g_t", "at_col", "sel_t", "e_cut", "selT", "v_t", "late", "att_a", "att_b", "a_max", "a_neg",
            "a_exp", "a_inv", "a3", "diag_t", "diag", "a_off", "a_t", "a_offT")}

        x_v = x.rearrange("(g b) (j p) d -> g j p b d", b=GB, p=P)
        out_v = out.rearrange("(g b) (j p) d -> g j p b d", b=GB, p=P)

        def parts(halved):
            return [(slice(it, it + 1), it) for it in range(T)] if halved else [(slice(0, T), 0)]

        def z_place(hop):
            return wide[1][:, :, (HOPS - hop) % 2, :]

        def last_t(it):
            return bank[2][it][:, 0:GB * P].unsqueeze(1)

        t_bank = [bank[0][0], bank[0][1], bank[2][0], bank[3][0]]

        block = ctx.enter_context(nc.Block())

        @block.sync
        def _(sp):
            for jt in range(T):
                sp.dma_start(x_all[:, 0, jt * GB:(jt + 1) * GB, :], x_v[0, jt]).then_inc(s_x, 16)
            sp.dma_start(w_raw[:], w_cheb).then_inc(s_w1, 16)
            for c in range(2):
                sp.dma_start(w10[:, c, :], w_pair[1 - c]).then_inc(s_l3w, 16)
            sp.dma_start(e_col[:], e_vals.rearrange("a t -> t a")).then_inc(s_l3w, 16)
            sp.dma_start(e_last[:], e_vals[0:1, NE - 1:NE].broadcast_to([P, 1])).then_inc(s_l3w, 16)
            sp.dma_start(bias_b[:], bias.rearrange("(a d) -> a d", a=1).broadcast_to([P, D])).then_inc(s_l3w, 16)
            sp.dma_start(others[:], w_others).then_inc(s_l2w, 16)
            sp.dma_start(w_selfs[:], w_self).then_inc(s_l2w, 16)
            sp.dma_start(att_cols[:], w_att.rearrange("(c p) a -> p (c a)", p=P),
                         allow_slow_non_contiguous=True).then_inc(s_l2w, 16)
            with sp.Fori(1, NG) as g:
                sp.wait_ge(s_x, g * 32)
                for jt in range(T):
                    sp.dma_start(x_all[:, g, jt * GB:(jt + 1) * GB, :], x_v[g, jt]).then_inc(s_x, 16)
            with sp.Fori(0, NG - 1) as g:
                sp.wait_ge(x_ok[3], g + 1)
                for jt in range(T):
                    sp.dma_start(out_v[g, jt], x_all[:, g, jt * GB:(jt + 1) * GB, :]).then_inc(s_out, 16)
            for jt in range(T):
                sp.wait_ge(x_ok[3], NG + jt)
                sp.dma_start(out_v[NG - 1, jt], x_all[:, NG - 1, jt * GB:(jt + 1) * GB, :]).then_inc(s_out, 16)
            sp.wait_ge(s_out, NG * T * 16)

        @block.gpsimd
        def _(pool):
            nc.gpsimd.memset(ident[:], 0.0).then_inc(s_ident, 1)
            nc.gpsimd.memset(minus_half[:], -0.5).then_inc(s_half, 1)
            nc.gpsimd.memset(minus_one[:], -1.0).then_inc(s_half, 1)
            nc.gpsimd.memset(eps_t[:], EPS).then_inc(s_half, 1)
            pool.wait_ge(s_ident, 1)
            nc.gpsimd.affine_select(out=ident[:], in_=ident[:], compare_op=ALU.not_equal, fill=1.0,
                                    base=0, pattern=[[-1, P]], channel_multiplier=1).then_inc(s_ident, 1)
            nc.gpsimd.memset(hv1[:, :, D:D + 1], 1.0).then_inc(setup["hv_ones"], 1)

            def inv_std(n, g):
                pool.wait_ge(meanvar_ok[n], g + 1)
                nc.gpsimd.tensor_tensor(var_eps[n][:], meanvar[n][:, :, 1], eps_t[:], ALU.add).then_inc(var_eps_ok[n], 1)
                if n == 0:
                    nc.gpsimd.tensor_tensor(minus_mean[:], meanvar[n][:, :, 0], minus_one[:], ALU.mult)
                pool.wait_ge(var_eps_ok[n], g + 1)
                nc.gpsimd.tensor_tensor(rstd[n][:], var_eps[n][:], minus_half[:], ALU.pow).then_inc(rstd_ok[n], 1)
                if n == 0:
                    pool.wait_ge(rstd_ok[n], g + 1)
                    nc.gpsimd.tensor_tensor(shift[:], minus_mean[:], rstd[n][:], ALU.mult).then_inc(shift_ok, 1)

            pool.wait_ge(s_half, 3)
            inv_std(0, 0)
            pool.wait_ge(s_w1, 16)
            nc.gpsimd.tensor_copy(w_hop[:, HOPS, :], w_raw[:, :, 0])
            for n in range(1, HOPS + 1):
                last = nc.gpsimd.tensor_tensor(w_hop[:, HOPS - n, :], w_raw[:, :, n], w_raw[:, :, n + HOPS], ALU.add)
            last.then_inc(setup["w_hop"], 1)
            nc.gpsimd.memset(ones[:], 1.0).then_inc(s_consts, 1)
            pool.wait_ge(s_consts, 1)
            nc.gpsimd.affine_select(out=before[:], in_=ones[:], compare_op=ALU.is_gt, fill=0.0, base=0,
                                    pattern=[[1, P]], channel_multiplier=-1)
            nc.gpsimd.iota(t_row[:], pattern=[[1, P]], base=0, channel_multiplier=0,
                           allow_small_or_imprecise_dtypes=True)
            nc.gpsimd.iota(t_one[:], pattern=[[0, 1]], base=1, channel_multiplier=1,
                           allow_small_or_imprecise_dtypes=True).then_inc(s_consts, 1)
            pool.wait_ge(s_l3w, 5 * 16)
            nc.gpsimd.affine_select(out=e_cut[:], in_=e_col[:], compare_op=ALU.not_equal, fill=0.0,
                                    base=-(NE - 1), pattern=[[0, 1]],
                                    channel_multiplier=1).then_inc(setup["e_cut"], 1)
            def off_diagonal():
                pool.wait_ge(setup["a3"], 1)
                for it in range(T):
                    nc.gpsimd.affine_select(out=a_off[:, it, :], in_=a3[:, it, :], compare_op=ALU.not_equal, fill=0.0,
                                            base=it * P, pattern=[[-1, N]],
                                            channel_multiplier=1).then_inc(setup["a_off"], 1)

            def masked(b, g):
                pool.wait_ge(exp_ok[b], g + 1)
                nc.gpsimd.tensor_tensor(pT[:, b], exp_s[:, b], adjT[:], ALU.mult).then_inc(pT_ok[b], 1)

            def weight_lows():
                pool.wait_ge(setup["w_hop_hi"], 1)
                nc.gpsimd.tensor_tensor(w_hop2[1][:], w_hop[:], w_hop2[0][:].bitcast(fp32),
                                        ALU.subtract).then_inc(setup["w_hop_lo"], 1)
                pool.wait_ge(setup["w10_hi"], 1)
                nc.gpsimd.tensor_tensor(w102[1][:], w10[:], w102[0][:].bitcast(fp32),
                                        ALU.subtract).then_inc(setup["w10_lo"], 1)

            def add_diagonal(g):
                pool.wait_ge(h0_diag_ok, g + 1)
                nc.gpsimd.tensor_tensor(h0_bias[:], h0_diag[:], bias_b[:].unsqueeze(1).broadcast_to([P, TG, D]),
                                        ALU.add).then_inc(h0_bias_ok, 1)
                pool.wait_ge(s_x, 32)
                pool.wait_ge(h0_bias_ok, g + 1)
                nc.gpsimd.tensor_tensor(x_all[:, g], x_all[:, g], h0_bias[:], ALU.add).then_inc(bias_ok, 1)

            def last_diagonal():
                x_g = x_all[:, NG - 1]
                pool.wait_ge(xn_ok[3], NG - 1 + T)
                nc.gpsimd.tensor_tensor(x_g, x_g, bias_b[:].unsqueeze(1).broadcast_to([P, TG, D]),
                                        ALU.add).then_inc(h0_bias_ok, 1)
                pool.wait_ge(h0_bias_ok, NG)
                for its, more in parts(True):
                    pool.wait_ge(h0_diag_ok, NG + more)
                    nc.gpsimd.tensor_tensor(by_it(x_g)[:, its], by_it(x_g)[:, its], by_it(h0_diag[:])[:, its],
                                            ALU.add).then_inc(bias_ok, 1)

            def pair_low(g):
                pool.wait_ge(hh_up_ok, g + 1)
                nc.gpsimd.tensor_tensor(hh_low[:], hh_up[:], w_low[:].unsqueeze(2).broadcast_to([P, TG, D]),
                                        ALU.mult).then_inc(hh_low_full, 1)
                pool.wait_ge(hh_low_hi, g + 1)
                nc.gpsimd.tensor_tensor(hh_low2[1][:], hh_low[:], hh_low2[0][:].bitcast(fp32),
                                        ALU.subtract).then_inc(hh_low_ok, 1)

            def body(s, layer3=True, next_group=True):
                masked(0, s)
                masked(1, s)
                if next_group:
                    inv_std(0, s + 1)
                inv_std(1, s)
                if layer3:
                    pair_low(s - 2)
                    add_diagonal(s - 3)
                inv_std(2, s - 1)
                inv_std(3, s - 2)

            inv_std(0, 1)
            pool.wait_ge(setup["adjT"], 1)
            masked(0, 0)
            masked(1, 0)
            weight_lows()
            inv_std(1, 0)
            inv_std(0, 2)
            masked(0, 1)
            masked(1, 1)
            off_diagonal()
            inv_std(1, 1)
            inv_std(2, 0)
            body(2, layer3=False)
            with pool.Fori(LAYERS - 1, NG - 1) as s:
                body(s)
            body(NG - 1, next_group=False)
            inv_std(2, NG - 1)
            add_diagonal(NG - 3)
            inv_std(3, NG - 2)
            inv_std(3, NG - 1)
            add_diagonal(NG - 2)
            last_diagonal()

        @block.scalar
        def _(act):
            act.dma_start(q_nat[:], q).then_inc(s_qk, 16)
            act.dma_start(k_nat[:], k).then_inc(s_qk, 16)
            act.dma_start(adj_nat[:], adj.rearrange("(t p) j -> p t j", p=P)).then_inc(s_adj, 16)
            act.dma_start(v_sb[:], v).then_inc(s_v, 16)

            def copy(out_ap, in_ap):
                return nc.scalar.activation(out_ap, in_ap, ACT.Copy)

            def normalise_0(g):
                act.wait_ge(s_x, 32)
                act.wait_ge(shift_ok, g + 1)
                for t in range(TG):
                    last = nc.scalar.activation(xn[0][:, t, :], x_all[:, g, t, :], ACT.Identity,
                                                bias=shift[:, t:t + 1], scale=rstd[0][:, t:t + 1])
                last.then_inc(xn_ok[0], 1)

            act.wait_ge(setup["qk_t"], 1)
            copy(qkT[:], tiles(bank[1][0][:, 0:2 * D], 2)).then_inc(setup["qkT"], 1)
            normalise_0(0)
            act.wait_ge(setup["m_t"], 1)
            copy(m_qk[:], bank[1][1][:, 0:D]).then_inc(setup["m_qk"], 1)

            def relu_t(n, g, src=None):
                act.wait_ge(t_done[n], g + 1)
                dst = hT2[n][0] if n in hT2 else hT[n]
                nc.scalar.activation(dst[:], tiles((src or t_bank[n])[:]), ACT.Relu).then_inc(hT_ok[n], 1)

            def last_relu_t():
                for its, more in parts(True):
                    act.wait_ge(t_done[3], NG + more)
                    nc.scalar.activation(by_it(hT2[3][0][:])[:, its], last_t(more), ACT.Relu).then_inc(hT_ok[3], 1)

            def setup_exp():
                act.wait_ge(setup["a_neg"], 1)
                for it in range(T):
                    nc.scalar.activation(a_exp[:, it, :], att_b[:, it, :], ACT.Exp, bias=a_neg[:, it:it + 1],
                                         accum_out=a_sum[:, it:it + 1]).then_inc(setup["a_exp"], 1)

            def scores(b, g):
                act.wait_ge(score_done[b], g + 1)
                nc.scalar.activation(tanh_s[:, b], tiles(bank[0][1 - b][:], T), ACT.Tanh,
                                     scale=SCORE_SCALE).then_inc(tanh_ok[b], 1)
                act.wait_ge(tanh_ok[b], g + 1)
                nc.scalar.activation(exp_s[:, b], tanh_s[:, b], ACT.Exp, scale=8.0).then_inc(exp_ok[b], 1)

            def high_part(n, g, halved=False):
                for its, more in parts(halved):
                    act.wait_ge(z_done[n + 1], g + 1 + more)
                    copy(by_it(z2[n][0][:])[:, its], z_place(n + 1)[:, its]).then_inc(z_hi_ok[n], 1)

            def copy_g(g):
                act.wait_ge(g_done, g + 1)
                copy(gT[:], tiles(bank[0][1][:])).then_inc(gT_ok, 1)

            def copy_hv(g):
                act.wait_ge(hv_done, g + 1)
                copy(hv1[:, :, 0:D], tiles(bank[0][0][:])).then_inc(hv_ok, 1)

            def pair_exps(g):
                act.wait_ge(neg_max_ok, g + 1)
                nc.scalar.activation(w_low[:], t_diff[:], ACT.Exp).then_inc(w_low_ok, 1)
                for t in range(TG):
                    last = nc.scalar.activation(p2[:, t, :], e_lr[:, t, :], ACT.Exp, bias=neg_max[:, t:t + 1],
                                                accum_out=up_sum[:, t:t + 1])
                last.then_inc(p2_ok, 1)

            def h1_high(g):
                act.wait_ge(h1_done, g + 1)
                copy(by_it(h12[0][:]), wide[3][:, :, 0, :]).then_inc(h1_hi_ok, 1)

            def h0_scaled(g):
                for it in range(T):
                    last = nc.scalar.activation(h0_diag[:, it * GB:(it + 1) * GB, :],
                                                wide[3][:, it, 1, :].rearrange("p (b d) -> p b d", b=GB),
                                                ACT.Copy, scale=diag[:, it:it + 1])
                last.then_inc(h0_diag_ok, 1)

            def last_h1():
                for its, more in parts(True):
                    act.wait_ge(h1_done, NG + more)
                    copy(by_it(h12[0][:])[:, its], wide[1][:, its, 0, :]).then_inc(h1_hi_ok, 1)
                act.wait_ge(bias_ok, NG - 1)
                for its, more in parts(True):
                    act.wait_ge(h1_ok, NG + more)
                    nc.scalar.activation(by_it(h0_diag[:])[:, its], wide[1][:, its, 1, :], ACT.Copy,
                                         scale=diag[:, its]).then_inc(h0_diag_ok, 1)

            def pair_low_high(g):
                act.wait_ge(hh_low_full, g + 1)
                copy(hh_low2[0][:], hh_low[:]).then_inc(hh_low_hi, 1)

            def body(s, layer3=True, next_group=True):
                if layer3:
                    copy_g(s)
                high_part(2, s - 1)
                if layer3:
                    copy_hv(s)
                scores(0, s)
                high_part(1, s - 1)
                relu_t(2, s - 2)
                scores(1, s)
                if layer3:
                    relu_t(3, s - 3)
                pair_exps(s - 2)
                if next_group:
                    act.wait_ge(t_done[0], s + 1)
                    normalise_0(s + 1)
                high_part(0, s - 1)
                if layer3:
                    h1_high(s - 3)
                    h0_scaled(s - 3)
                pair_low_high(s - 2)
                if next_group:
                    relu_t(0, s + 1)
                relu_t(1, s)

            relu_t(0, 0)
            copy_g(0)
            copy_hv(0)
            scores(0, 0)
            scores(1, 0)
            act.wait_ge(setup["adjT"], 1)
            copy(adjT2[0][:], adjT[:]).then_inc(setup["adjT_hi"], 1)
            act.wait_ge(setup["low_mask"], 1)
            copy(low_mask_r[:], low_mask[:]).then_inc(setup["low_mask_r"], 1)
            act.wait_ge(setup["w_hop"], 1)
            copy(w_hop2[0][:], w_hop[:]).then_inc(setup["w_hop_hi"], 1)
            act.wait_ge(t_done[0], 1)
            normalise_0(1)
            act.wait_ge(s_l3w, 5 * 16)
            copy(w102[0][:], w10[:]).then_inc(setup["w10_hi"], 1)
            relu_t(0, 1)
            copy_g(1)
            copy_hv(1)
            relu_t(1, 0, bank[1][0])
            high_part(2, 0)
            scores(0, 1)
            act.wait_ge(t_done[0], 2)
            normalise_0(2)
            high_part(1, 0)
            scores(1, 1)
            setup_exp()
            high_part(0, 0)
            relu_t(0, 2)
            copy_g(2)
            copy_hv(2)
            relu_t(1, 1, bank[1][0])
            act.wait_ge(setup["a_offT"], 1)
            copy(a_offT2[0][:], a_offT[:]).then_inc(setup["a_offT_hi"], 1)
            body(2, layer3=False)
            with act.Fori(LAYERS - 1, NG - 1) as s:
                body(s)
            body(NG - 1, next_group=False)
            high_part(2, NG - 1, halved=True)
            high_part(1, NG - 1, halved=True)
            relu_t(2, NG - 2)
            high_part(0, NG - 1, halved=True)
            relu_t(3, NG - 3)
            pair_exps(NG - 2)
            h1_high(NG - 3)
            h0_scaled(NG - 3)
            pair_low_high(NG - 2)
            relu_t(2, NG - 1)
            pair_exps(NG - 1)
            relu_t(3, NG - 2)
            pair_low_high(NG - 1)
            h1_high(NG - 2)
            h0_scaled(NG - 2)
            last_relu_t()
            last_h1()

        @block.vector
        def _(dve):
            def wait_alone(s, n):
                dve.wait_ge(s_x, 32)
                dve.wait_ge(s, n)

            def moments(n, g, ready, count):
                wait_alone(ready, count)
                for t in range(TG):
                    last = nc.vector.bn_stats(stats[n][:, t, :], x_all[:, g, t, :])
                first = n == 0 and isinstance(g, int) and g == 0
                seen, at = (setup["first_stats"], 1) if first else (stats_seen[n], g if n == 0 else g + 1)
                last.then_inc(seen, 1)
                wait_alone(seen, at)
                for t in range(TG):
                    last = nc.vector.bn_aggr(meanvar[n][:, t, :], stats[n][:, t, :])
                last.then_inc(meanvar_ok[n], 1)

            def normalise(n, g, halved=False):
                dve.wait_ge(rstd_ok[n], g + 1)
                for t in range(TG):
                    if halved and t == GB:
                        last.then_inc(xn_ok[n], 1)
                    last = nc.vector.tensor_scalar(xn[n][:, t, :], x_all[:, g, t, :], meanvar[n][:, t, 0:1],
                                                   rstd[n][:, t:t + 1], ALU.subtract, ALU.mult)
                last.then_inc(xn_ok[n], 1)

            def adjacency():
                dve.wait_ge(setup["adj_t"], 1)
                nc.vector.tensor_copy(adjT[:], tiles(bank[0][1][:], T)).then_inc(setup["adjT"], 1)

            def adjacency_low():
                dve.wait_ge(setup["adjT_hi"], 1)
                nc.vector.tensor_tensor(adjT2[1][:], adjT[:], adjT2[0][:].bitcast(fp32),
                                        ALU.subtract).then_inc(setup["adjT_lo"], 1)

            def pair_bounds():
                dve.wait_ge(setup["adjT"], 1)
                nc.vector.tensor_scalar(up_bound[:], adjT[:, :, 0:P], 0.0, HUGE, ALU.is_gt,
                                        ALU.mult).then_inc(setup["up1"], 1)
                nc.vector.tensor_scalar(low_mask[:], adjT[:, :, P:N], 0.0, None,
                                        ALU.is_gt).then_inc(setup["low_raw"], 1)
                dve.wait_ge(setup["up1"], 1)
                nc.vector.tensor_reduce(any_up[:], up_bound[:], axis=AX.X, op=ALU.max)
                dve.wait_ge(setup["low_raw"], 1)
                nc.vector.tensor_reduce(any_low[:], low_mask[:], axis=AX.X, op=ALU.max).then_inc(setup["any"], 1)
                dve.wait_ge(setup["any"], 1)
                nc.vector.tensor_tensor(edgeless[:], any_up[:], any_low[:], ALU.max).then_inc(setup["some"], 1)
                nc.vector.tensor_scalar(low_bound[:], any_low[:], HUGE, NEG_PRE, ALU.mult, ALU.add)
                nc.vector.tensor_scalar(up_bound[:], up_bound[:], NEG_PRE, None, ALU.add)
                dve.wait_ge(setup["some"], 1)
                nc.vector.tensor_scalar(edgeless[:], edgeless[:], 0.0, None,
                                        ALU.is_le).then_inc(setup["edgeless"], 1)
                dve.wait_ge(setup["edgeless"], 1)
                for jt in range(T):
                    last = nc.vector.tensor_scalar(low_mask[:, jt, :], low_mask[:, jt, :], edgeless[:, jt:jt + 1],
                                                   None, ALU.max)
                last.then_inc(setup["low_mask"], 1)
                dve.wait_ge(setup["low_mask"], 1)
                nc.vector.tensor_reduce(low_count[:], low_mask[:], axis=AX.X, op=ALU.add)

            def pair_vectors():
                dve.wait_ge(setup["u_t"], 1)
                nc.vector.tensor_copy(u_cols[:], bank[2][1][:, 0:2]).then_inc(setup["u_cols"], 1)
                dve.wait_ge(setup["u_cols"], 1)
                nc.vector.tensor_scalar(u_sum[:], u_cols[:, 0:1].broadcast_to([P, P]), u_cols[:, 1:2], None,
                                        ALU.add).then_inc(setup["u_sum"], 1)

            def edge_counts():
                dve.wait_ge(s_adj, 16)
                nc.vector.tensor_scalar(mask3[:], adj_nat[:], 0.0, None, ALU.is_gt).then_inc(setup["mask3"], 1)
                dve.wait_ge(setup["mask3"], 1)
                for it in range(T):
                    last = nc.vector.tensor_tensor_scan(cum[:, it, :], mask3[:, it, :], mask3[:, it, :], 0.0,
                                                        ALU.add, ALU.max)
                last.then_inc(setup["cum"], 1)
                nc.vector.tensor_scalar(not_edge[:], mask3[:], 1.0, -NEG, ALU.subtract, ALU.mult)
                dve.wait_ge(setup["cum"], 1)
                nc.vector.tensor_copy(row_tot[:], cum[:, :, N - 1]).then_inc(setup["row_tot"], 1)

            def edge_rows():
                dve.wait_ge(setup["base_t"], 1)
                nc.vector.tensor_copy(row_base[:], bank[3][0][:, 0:T]).then_inc(setup["row_base"], 1)
                dve.wait_ge(setup["row_base"], 1)
                nc.vector.tensor_tensor(row_end[:], row_base[:], row_tot[:], ALU.add).then_inc(setup["row_end"], 1)
                for it in range(T):
                    last = nc.vector.scalar_tensor_tensor(rank[:, it, :], cum[:, it, :], row_base[:, it:it + 1],
                                                          mask3[:, it, :], ALU.add, ALU.mult)
                last.then_inc(setup["rank"], 1)
                dve.wait_ge(s_consts, 2)
                dve.wait_ge(setup["row_end"], 1)
                for it in range(T):
                    last = nc.vector.tensor_scalar(ended[:, it, :], t_row[:], row_end[:, it:it + 1], None, ALU.is_lt)
                last.then_inc(setup["ended"], 1)
                dve.wait_ge(setup["ended"], 1)
                for it in range(T):
                    last = nc.vector.scalar_tensor_tensor(sel[:, it, :], t_row[:], row_base[:, it:it + 1],
                                                          ended[:, it, :], ALU.is_ge, ALU.mult)
                last.then_inc(setup["sel"], 1)
                dve.wait_ge(s_l3w, 5 * 16)
                dve.wait_ge(setup["rank"], 1)
                nc.vector.tensor_scalar(late[:], rank[:], float(NE), e_last[:, 0:1], ALU.is_ge,
                                        ALU.mult).then_inc(setup["late"], 1)

            def edge_columns():
                dve.wait_ge(setup["g_t"], 1)
                nc.vector.tensor_scalar(at_col[:], bank[3][0][:, 0:N], t_one[:, 0:1], None,
                                        ALU.is_equal).then_inc(setup["at_col"], 1)
                dve.wait_ge(setup["e_cut"], 1)
                dve.wait_ge(setup["sel_t"], 1)
                nc.vector.tensor_scalar(selT[:], tiles(bank[3][1][:, 0:N], T), e_cut[:, 0:1], None,
                                        ALU.mult).then_inc(setup["selT"], 1)

            def edge_values():
                dve.wait_ge(setup["v_t"], 1)
                dve.wait_ge(setup["late"], 1)
                nc.vector.tensor_tensor(att_a[:], tiles(bank[3][0][:], T), late[:], ALU.add).then_inc(setup["att_a"], 1)
                dve.wait_ge(setup["att_a"], 1)
                nc.vector.tensor_tensor(att_b[:], att_a[:], not_edge[:], ALU.add).then_inc(setup["att_b"], 1)
                dve.wait_ge(setup["att_b"], 1)
                nc.vector.tensor_reduce(a_max[:], att_b[:], axis=AX.X, op=ALU.max).then_inc(setup["a_max"], 1)
                dve.wait_ge(setup["a_max"], 1)
                nc.vector.tensor_scalar(a_neg[:], a_max[:], -1.0, None, ALU.mult).then_inc(setup["a_neg"], 1)

            def edge_softmax():
                dve.wait_ge(setup["a_exp"], T)
                nc.vector.reciprocal(a_inv[:], a_sum[:]).then_inc(setup["a_inv"], 1)
                dve.wait_ge(setup["a_inv"], 1)
                for it in range(T):
                    last = nc.vector.tensor_scalar(a3[:, it, :], a_exp[:, it, :], a_inv[:, it:it + 1], None, ALU.mult)
                last.then_inc(setup["a3"], 1)
                dve.wait_ge(setup["a3"], 1)
                for it in range(T):
                    last = nc.vector.tensor_tensor(diag_t[:, it, :], a3[:, it, it * P:(it + 1) * P], ident[:], ALU.mult)
                last.then_inc(setup["diag_t"], 1)
                dve.wait_ge(setup["diag_t"], 1)
                nc.vector.tensor_reduce(diag[:], diag_t[:], axis=AX.X, op=ALU.add).then_inc(setup["diag"], 1)

            def edge_transposed():
                dve.wait_ge(setup["a_t"], 1)
                nc.vector.tensor_copy(a_offT[:], tiles(bank[3][0][:], T)).then_inc(setup["a_offT"], 1)

            def edge_transposed_low():
                dve.wait_ge(setup["a_offT_hi"], 1)
                nc.vector.tensor_tensor(a_offT2[1][:], a_offT[:], a_offT2[0][:].bitcast(fp32),
                                        ALU.subtract).then_inc(setup["a_offT_lo"], 1)

            def add_to_x(n, g, src, its=slice(0, T)):
                x_g = by_it(x_all[:, g])[:, its] if n in wide else x_all[:, g]
                nc.vector.tensor_tensor(x_g, src, x_g, ALU.add).then_inc(x_ok[n], 1)

            def pair_scores(g):
                dve.wait_ge(s_done, g + 1)
                nc.vector.tensor_tensor(e_min[:].rearrange("p (j b) i -> p j b i", j=T),
                                        bank[2][1][:].rearrange("p (j b i) -> p j b i", j=T, b=GB),
                                        up_bound[:].unsqueeze(2).broadcast_to([P, T, GB, P]),
                                        ALU.min).then_inc(e_min_ok, 1)
                dve.wait_ge(pair_done, g + 1)
                nc.vector.tensor_tensor(t_min[:].rearrange("p (j b) -> p j b", j=T),
                                        bank[0][1][:, CH - GB:CH].unsqueeze(1).broadcast_to([P, T, GB]),
                                        low_bound[:].unsqueeze(2).broadcast_to([P, T, GB]),
                                        ALU.min).then_inc(t_min_ok, 1)
                dve.wait_ge(e_min_ok, g + 1)
                nc.vector.scalar_tensor_tensor(e_lr[:], e_min[:], SLOPE, e_min[:], ALU.mult,
                                               ALU.max).then_inc(e_lr_ok, 1)
                dve.wait_ge(e_lr_ok, g + 1)
                nc.vector.tensor_reduce(e_max[:], e_lr[:], axis=AX.X, op=ALU.max).then_inc(e_max_ok, 1)
                dve.wait_ge(t_min_ok, g + 1)
                nc.vector.scalar_tensor_tensor(t_lr[:], t_min[:], SLOPE, t_min[:], ALU.mult,
                                               ALU.max).then_inc(t_lr_ok, 1)
                dve.wait_ge(e_max_ok, g + 1)
                dve.wait_ge(t_lr_ok, g + 1)
                nc.vector.tensor_tensor(j_max[:], e_max[:], t_lr[:], ALU.max).then_inc(j_max_ok, 1)
                dve.wait_ge(j_max_ok, g + 1)
                nc.vector.tensor_tensor(t_diff[:], t_lr[:], j_max[:], ALU.subtract)
                nc.vector.tensor_scalar(neg_max[:], j_max[:], -1.0, None, ALU.mult).then_inc(neg_max_ok, 1)

            def pair_sums(g):
                dve.wait_ge(w_low_ok, g + 1)
                nc.vector.tensor_tensor(low_sum[:].rearrange("p (j b) -> p j b", j=T),
                                        w_low[:].rearrange("p (j b) -> p j b", j=T),
                                        low_count[:].unsqueeze(2).broadcast_to([P, T, GB]),
                                        ALU.mult).then_inc(low_sum_ok, 1)
                dve.wait_ge(low_sum_ok, g + 1)
                dve.wait_ge(p2_ok, g + 1)
                nc.vector.tensor_tensor(all_sum[:], low_sum[:], up_sum[:], ALU.add).then_inc(all_sum_ok, 1)
                dve.wait_ge(all_sum_ok, g + 1)
                nc.vector.reciprocal(col_inv[:], all_sum[:]).then_inc(col_inv_ok, 1)
                dve.wait_ge(col_inv_ok, g + 1)
                dve.wait_ge(hh_done, g + 1)
                nc.vector.tensor_tensor(hh_up[:], tiles(bank[2][0][:]),
                                        col_inv[:].unsqueeze(2).broadcast_to([P, TG, D]),
                                        ALU.mult).then_inc(hh_up_ok, 1)

            def pair_low_full(g):
                dve.wait_ge(hh_up_ok, g + 1)
                nc.vector.tensor_tensor(hh_low[:], hh_up[:], w_low[:].unsqueeze(2).broadcast_to([P, TG, D]),
                                        ALU.mult).then_inc(hh_low_full, 1)

            def pair_low_rest(g):
                dve.wait_ge(hh_low_hi, g + 1)
                nc.vector.tensor_tensor(hh_low2[1][:], hh_low[:], hh_low2[0][:].bitcast(fp32),
                                        ALU.subtract).then_inc(hh_low_ok, 1)

            def low_part(pair, src, hi_ok, ok, g, halved=False):
                for its, more in parts(halved):
                    dve.wait_ge(hi_ok, g + 1 + more)
                    nc.vector.tensor_tensor(by_it(pair[1][:])[:, its], src[:, its],
                                            by_it(pair[0][:].bitcast(fp32))[:, its], ALU.subtract).then_inc(ok, 1)

            def last_relu_low():
                for its, more in parts(True):
                    dve.wait_ge(hT_ok[3], NG + more)
                    nc.vector.scalar_tensor_tensor(by_it(hT2[3][1][:])[:, its], last_t(more), 0.0,
                                                   by_it(hT2[3][0][:].bitcast(fp32))[:, its], ALU.max,
                                                   ALU.subtract).then_inc(hT_low_ok[3], 1)

            def relu_low(n, g, src=None):
                dve.wait_ge(hT_ok[n], g + 1)
                nc.vector.scalar_tensor_tensor(hT2[n][1][:], tiles((src or t_bank[n])[:]), 0.0,
                                               hT2[n][0][:].bitcast(fp32), ALU.max,
                                               ALU.subtract).then_inc(hT_low_ok[n], 1)

            def attention_out(g):
                for b in range(GB):
                    dve.wait_ge(o_done[b], g + 1)
                    o = bank[0][1 - b][:, 0:T * (D + 1)].rearrange("p (i d) -> p i d", i=T)
                    nc.vector.reciprocal(row_inv[:, b, :], o[:, :, D]).then_inc(row_inv_ok[b], 1)
                    dve.wait_ge(row_inv_ok[b], g + 1)
                    for it in range(T):
                        t = it * GB + b
                        last = nc.vector.scalar_tensor_tensor(x_all[:, g, t, :], o[:, it, 0:D],
                                                              row_inv[:, b, it:it + 1], x_all[:, g, t, :],
                                                              ALU.mult, ALU.add)
                last.then_inc(x_ok[0], 1)

            def z_low(n, g, halved=False):
                low_part(z2[n], z_place(n + 1), z_hi_ok[n], z_ok[n], g, halved)

            def h1_low(g):
                dve.wait_ge(h0_diag_ok, g + 1)
                low_part(h12, wide[3][:, :, 0, :], h1_hi_ok, h1_ok, g)

            def layer1_out(g, halved=False):
                for its, more in parts(halved):
                    dve.wait_ge(z_done[0], g + 1 + more)
                    add_to_x(1, g, z_place(0)[:, its], its)

            def layer2_out(g):
                dve.wait_ge(out2_done, g + 1)
                add_to_x(2, g, tiles(bank[2][1][:]))

            def layer3_out(g, halved=False):
                for its, more in parts(halved):
                    dve.wait_ge(bias_ok, g + 1 + more)
                    dve.wait_ge(out3_done, g + 1 + more)
                    add_to_x(3, g, wide[1 if halved else 3][:, its, 0, :], its)

            def body(s, layer3=True, next_group=True):
                if layer3:
                    normalise(3, s - 3)
                z_low(1, s - 1)
                if next_group:
                    moments(0, s + 1, s_x, s * 32 + 64)
                pair_scores(s - 2)
                if layer3:
                    relu_low(3, s - 3)
                attention_out(s)
                pair_sums(s - 2)
                moments(1, s, x_ok[0], s + 1)
                z_low(0, s - 1)
                if layer3:
                    h1_low(s - 3)
                else:
                    pair_low_full(s - 2)
                normalise(1, s)
                if not layer3:
                    pair_low_rest(s - 2)
                layer1_out(s - 1)
                relu_low(1, s)
                moments(2, s - 1, x_ok[1], s)
                layer2_out(s - 2)
                if next_group:
                    moments(3, s - 2, x_ok[2], s - 1)
                z_low(2, s, halved=not next_group)
                normalise(2, s - 1)
                if not next_group:
                    z_low(1, s, halved=True)
                    moments(3, s - 2, x_ok[2], s - 1)
                if layer3:
                    layer3_out(s - 3)

            moments(0, 0, s_x, 32)
            adjacency()
            edge_counts()
            dve.wait_ge(xn_ok[0], 1)
            moments(0, 1, s_x, 64)
            pair_bounds()
            edge_rows()
            attention_out(0)
            moments(1, 0, x_ok[0], 1)
            dve.wait_ge(setup["oth_t"], 1)
            nc.vector.tensor_copy(othersT[:], bank[2][0][:, 0:D]).then_inc(setup["othersT"], 1)
            edge_columns()
            adjacency_low()
            normalise(1, 0)
            moments(0, 2, s_x, 96)
            pair_vectors()
            relu_low(1, 0, bank[1][0])
            edge_values()
            z_low(2, 0)
            z_low(1, 0)
            edge_softmax()
            z_low(0, 0)
            attention_out(1)
            moments(1, 1, x_ok[0], 2)
            layer1_out(0)
            moments(2, 0, x_ok[1], 1)
            normalise(1, 1)
            edge_transposed()
            relu_low(1, 1, bank[1][0])
            normalise(2, 0)
            z_low(2, 1)
            edge_transposed_low()
            body(2, layer3=False)
            with dve.Fori(LAYERS - 1, NG - 1) as s:
                body(s)
            body(NG - 1, next_group=False)
            normalise(3, NG - 3)
            z_low(0, NG - 1, halved=True)
            pair_scores(NG - 2)
            layer1_out(NG - 1, halved=True)
            relu_low(3, NG - 3)
            moments(2, NG - 1, x_ok[1], NG + 1)
            pair_sums(NG - 2)
            normalise(2, NG - 1)
            pair_low_full(NG - 2)
            pair_low_rest(NG - 2)
            h1_low(NG - 3)
            layer2_out(NG - 2)
            moments(3, NG - 2, x_ok[2], NG - 1)
            pair_scores(NG - 1)
            normalise(3, NG - 2)
            layer3_out(NG - 3)
            pair_sums(NG - 1)
            pair_low_full(NG - 1)
            relu_low(3, NG - 2)
            pair_low_rest(NG - 1)
            layer2_out(NG - 1)
            moments(3, NG - 1, x_ok[2], NG)
            h1_low(NG - 2)
            normalise(3, NG - 1, halved=True)
            last_relu_low()
            layer3_out(NG - 2)
            low_part(h12, wide[1][:, :, 0, :], h1_hi_ok, h1_ok, NG - 1, halved=True)
            layer3_out(NG - 1, halved=True)

        @block.tensor
        def _(pe):
            def mm(o, lhsT, rhs, start=True, stop=True, shared=False):
                return nc.tensor.matmul(o, lhsT, rhs, start=start, stop=stop, skip_group_check=shared)

            def transposes(n, g, to_bank=None):
                pe.wait_ge(xn_ok[n], g + 1)
                bk = tiles((to_bank or t_bank[n])[:])
                for t in range(TG):
                    to = t % GB * T + t // GB if n == 2 else t
                    last = nc.tensor.transpose(bk[:, to, :], xn[n][:, t, :], ident[:])
                last.then_inc(t_done[n], 1)

            def keep_clock(n):
                for _ in range(n):
                    mm(bank[0][0][:], low_mask_r[:, 0, :], adjT2[0][:].rearrange("p j i -> p (j i)"))

            def raise_clock(n):
                for _ in range(n):
                    mm(bank[2][0][:, 0:P], ident[:], ident[:])

            def bank_read(s, n):
                if not isinstance(n, int) or n > 0:
                    pe.wait_ge(s, n)

            def mm_split(o, lhsT2, rhs2, start, stop):
                pairs = [(0, 0), (0, 1), (1, 0)][:3 if len(lhsT2) == 2 else 2]
                for n, (c, d) in enumerate(pairs):
                    last = mm(o, lhsT2[c], rhs2[d], start=start and n == 0, stop=stop and n == len(pairs) - 1,
                              shared=True)
                return last

            def two_products(n, w2, c, its=range(T), place=None):
                for it in its:
                    for b in range(GB):
                        t = it * GB + b
                        o = wide[place or n][:, it].rearrange("p c (b d) -> p b c d", b=GB)[:, b]
                        last = mm_split(o, [h[:, t, :] for h in hT2[n]], [w[:, c:c + 2, :] for w in w2],
                                        b == 0, False)
                return last

            def horner_adj(hop, it):
                for jt in range(T):
                    last = mm_split(z_place(hop)[:, it, :], [a[:, jt, it * P:(it + 1) * P] for a in adjT2],
                                    [p[:, jt * GB:(jt + 1) * GB, :] for p in z2[hop]], False, jt == T - 1)
                return last

            def scores(b, g):
                gv = gT[:].rearrange("p (i b) d -> p i b d", b=GB)
                for jt in range(T):
                    last = mm(tiles(bank[0][1 - b][:], T)[:, jt, :].rearrange("p (i d) -> p i d", i=T),
                              hT[0][:, jt * GB + b, :], gv[:, :, b, :])
                last.then_inc(score_done[b], 1)

            def project_g(g):
                pe.wait_ge(hT_ok[0], g + 1)
                if not isinstance(g, int) or g > 2:
                    pe.wait_ge(hT_low_ok[1], g)
                mm(bank[0][1][:], m_qk[:], hT[0][:].rearrange("p t d -> p (t d)")).then_inc(g_done, 1)

            def project_v(g):
                for t in range(TG):
                    last = mm(tiles(bank[0][0][:])[:, t, :], hT[0][:, t, :], v_sb[:])
                last.then_inc(hv_done, 1)

            def scores_0(g):
                pe.wait_ge(gT_ok, g + 1)
                scores(0, g)

            def scores_1(g):
                pe.wait_ge(hv_ok, g + 1)
                scores(1, g)

            def attend(g):
                if not isinstance(g, int) or g > 1:
                    pe.wait_ge(t_min_ok, g - 1)
                for b in range(GB):
                    pe.wait_ge(pT_ok[b], g + 1)
                    o = bank[0][1 - b][:, 0:T * (D + 1)].rearrange("p (i d) -> p i d", i=T)
                    for it in range(T):
                        for jt in range(T):
                            last = mm(o[:, it, :], pT[:, b, jt, it * P:(it + 1) * P], hv1[:, jt * GB + b, :],
                                      start=jt == 0, stop=jt == T - 1)
                    last.then_inc(o_done[b], 1)

            def horner_32(g, halved=False):
                pe.wait_ge(hT_low_ok[1], g + 1)
                bank_read(x_ok[1], g)
                for its, _ in parts(halved):
                    two_products(1, w_hop2, 0, range(T)[its]).then_inc(z_done[HOPS], 1)

            def hop(n, g, halved, started=False):
                if not started:
                    pe.wait_ge(z_ok[n], g + T if halved else g + 1)
                for its, _ in parts(halved):
                    for it in range(T)[its]:
                        last = horner_adj(n, it)
                    last.then_inc(z_done[n], 1)

            def horner_2(g, halved=False):
                hop(2, g, halved)

            def horner_1(g, halved=False):
                for its, more in parts(halved):
                    pe.wait_ge(z_ok[1], g + 1 + more)
                    two_products(1, w_hop2, 2, range(T)[its])
                hop(1, g, halved, started=True)

            def horner_0(g, halved=False):
                hop(0, g, halved)

            def pair_products(g, lent, count):
                pe.wait_ge(hT_ok[2], g + 1)
                bank_read(x_ok[2], g)
                pairs = hT[2][:].rearrange("p (b i) (c r) -> p r b (i c)", b=GB, r=2)
                mm(bank[2][1][:].rearrange("p (j b i) -> p j b i", j=T, b=GB), u_sum[:], pairs).then_inc(s_done, 1)
                pe.wait_ge(lent, count)
                for b in range(GB):
                    for r in range(2):
                        last = mm(bank[0][1][:, CH - GB + b:CH - GB + b + 1], pairs[:, r, b, :], u_cols[:, r:r + 1],
                                  start=r == 0, stop=r == 1)
                last.then_inc(pair_done, 1)
                for t in range(TG):
                    last = mm(tiles(bank[2][0][:])[:, t, :], hT[2][:, t % GB * T + t // GB, :], others[:])
                last.then_inc(hh_done, 1)

            def pair_self(g):
                pe.wait_ge(e_min_ok, g + 1)
                for it in range(T):
                    for b in range(GB):
                        mm(tiles(bank[2][1][:])[:, it * GB + b, :], hT[2][:, b * T + it, :], w_selfs[:],
                           start=it == 0 and b == 0, stop=False, shared=True)

            def pair_upper(g):
                pe.wait_ge(p2_ok, g + 1)
                pe.wait_ge(hh_up_ok, g + 1)
                for b in range(GB):
                    for jt in range(T):
                        mm(tiles(bank[2][1][:])[:, b, :], p2[:, jt * GB + b, :], hh_up[:, jt * GB + b, :],
                           start=False, stop=jt == T - 1, shared=True)

            def pair_lower(g):
                o = tiles(bank[2][1][:])
                pe.wait_ge(hh_low_ok, g + 1)
                for jt in range(T):
                    last = mm_split(o[:, GB:2 * GB, :], [low_mask_r[:, jt, :]],
                                    [p[:, jt * GB:(jt + 1) * GB, :] for p in hh_low2], False, jt == T - 1)
                last.then_inc(out2_done, 1)

            def learnt_h(g):
                pe.wait_ge(hT_low_ok[3], g + 1)
                two_products(3, w102, 0).then_inc(h1_done, 1)

            def off_diagonal_rows(it, place=3):
                for jt in range(T):
                    last = mm_split(wide[place][:, it, 0, :], [a[:, jt, it * P:(it + 1) * P] for a in a_offT2],
                                    [p[:, jt * GB:(jt + 1) * GB, :] for p in h12], jt == 0, jt == T - 1)
                return last

            def learnt_out(g):
                pe.wait_ge(h1_ok, g + 1)
                for it in range(T):
                    last = off_diagonal_rows(it)
                last.then_inc(out3_done, 1)

            def transposes_3(g):
                bank_read(x_ok[3], g)
                transposes(3, g)

            def last_transposes_3():
                for it in range(T):
                    pe.wait_ge(xn_ok[3], NG + it)
                    for b in range(GB):
                        last = nc.tensor.transpose(last_t(it)[:, 0, b * P:(b + 1) * P], xn[3][:, it * GB + b, :],
                                                   ident[:])
                    last.then_inc(t_done[3], 1)

            def last_learnt():
                for it in range(T):
                    pe.wait_ge(hT_low_ok[3], NG + it)
                    two_products(3, w102, 0, [it], place=1).then_inc(h1_done, 1)
                keep_clock(4)
                pe.wait_ge(h1_ok, NG - 1 + T)
                for it in range(T):
                    pe.wait_ge(h0_diag_ok, NG + it)
                    off_diagonal_rows(it, place=1).then_inc(out3_done, 1)

            def body(s, layer3=True, next_group=True):
                if layer3:
                    project_g(s)
                horner_32(s - 1)
                if layer3:
                    project_v(s)
                scores_0(s)
                horner_2(s - 1)
                transposes(2, s - 2)
                scores_1(s)
                if layer3:
                    transposes_3(s - 3)
                pair_products(s - 2, tanh_ok[0], s + 1)
                attend(s)
                horner_1(s - 1)
                if layer3:
                    learnt_h(s - 3)
                pair_self(s - 2)
                pair_upper(s - 2)
                if next_group:
                    pe.wait_ge(x_ok[0], s + 1)
                    transposes(0, s + 1)
                horner_0(s - 1)
                transposes(1, s)
                if layer3:
                    learnt_out(s - 3)
                pair_lower(s - 2)

            pe.wait_ge(s_ident, 2)
            raise_clock(8)
            pe.wait_ge(s_qk, 32)
            bk = tiles(bank[1][0][:, 0:2 * D], 2)
            nc.tensor.transpose(bk[:, 0, :], q_nat[:], ident[:])
            nc.tensor.transpose(bk[:, 1, :], k_nat[:], ident[:]).then_inc(setup["qk_t"], 1)
            raise_clock(6)
            pe.wait_ge(s_adj, 16)
            bk = tiles(bank[0][1][:], T)
            for it in range(T):
                for jt in range(T):
                    last = nc.tensor.transpose(bk[:, jt, it * P:(it + 1) * P], adj_nat[:, it, jt * P:(jt + 1) * P],
                                               ident[:])
            last.then_inc(setup["adj_t"], 1)
            pe.wait_ge(setup["qkT"], 1)
            mm(bank[1][1][:, 0:D], qkT[:, 0, :], qkT[:, 1, :]).then_inc(setup["m_t"], 1)
            raise_clock(4)
            transposes(0, 0)
            raise_clock(3)
            for n in ("adjT", "m_qk", "hv_ones"):
                pe.wait_ge(setup[n], 1)
            pe.wait_ge(s_v, 16)
            project_g(0)
            project_v(0)
            scores_0(0)
            scores_1(0)
            pe.wait_ge(setup["row_tot"], 1)
            pe.wait_ge(s_consts, 2)
            mm(bank[3][0][:, 0:1], before[:], row_tot[:, 0:1])
            mm(bank[3][0][:, 1:2], ones[:], row_tot[:, 0:1], stop=False)
            mm(bank[3][0][:, 1:2], before[:], row_tot[:, 1:2], start=False).then_inc(setup["base_t"], 1)
            pe.wait_ge(s_l2w, 48)
            nc.tensor.transpose(bank[2][0][:, 0:D], others[:], ident[:]).then_inc(setup["oth_t"], 1)
            attend(0)
            pe.wait_ge(setup["sel"], 1)
            pe.wait_ge(setup["rank"], 1)
            pe.wait_ge(setup["row_base"], 1)
            for it in range(T):
                last = mm(bank[3][0][:, 0:N], sel[:, it, :], rank[:, it, :], start=it == 0, stop=it == T - 1)
            last.then_inc(setup["g_t"], 1)
            for it in range(T):
                last = nc.tensor.transpose(bank[3][1][:, it * P:(it + 1) * P], sel[:, it, :], ident[:])
            last.then_inc(setup["sel_t"], 1)
            pe.wait_ge(x_ok[0], 1)
            transposes(0, 1)
            project_g(1)
            project_v(1)
            pe.wait_ge(setup["othersT"], 1)
            mm(bank[2][1][:, 0:2], othersT[:], att_cols[:]).then_inc(setup["u_t"], 1)
            pe.wait_ge(setup["at_col"], 1)
            pe.wait_ge(setup["selT"], 1)
            for it in range(T):
                last = mm(bank[3][0][:, it * N:(it + 1) * N], selT[:, it, :], at_col[:])
            last.then_inc(setup["v_t"], 1)
            raise_clock(2)
            transposes(1, 0, bank[1][0])
            raise_clock(3)
            for n in ("w_hop_hi", "w_hop_lo", "adjT_hi", "adjT_lo"):
                pe.wait_ge(setup[n], 1)
            horner_32(0)
            scores_0(1)
            raise_clock(2)
            horner_2(0)
            scores_1(1)
            horner_1(0)
            attend(1)
            horner_0(0)
            pe.wait_ge(setup["a_off"], T)
            pe.wait_ge(setup["att_a"], 1)
            bk = tiles(bank[3][0][:], T)
            for it in range(T):
                for jt in range(T):
                    last = nc.tensor.transpose(bk[:, jt, it * P:(it + 1) * P], a_off[:, it, jt * P:(jt + 1) * P],
                                               ident[:])
            last.then_inc(setup["a_t"], 1)
            raise_clock(4)
            pe.wait_ge(x_ok[0], 2)
            transposes(0, 2)
            raise_clock(2)
            project_g(2)
            project_v(2)
            pe.wait_ge(x_ok[1], 1)
            transposes(1, 1, bank[1][0])
            raise_clock(4)
            pe.wait_ge(setup["u_sum"], 1)
            pe.wait_ge(setup["low_mask_r"], 1)
            body(2, layer3=False)
            for n in ("a_offT_hi", "a_offT_lo", "w10_hi", "w10_lo"):
                pe.wait_ge(setup[n], 1)
            with pe.Fori(LAYERS - 1, NG - 1) as s:
                body(s)
            body(NG - 1, next_group=False)
            horner_32(NG - 1, halved=True)
            keep_clock(4)
            horner_2(NG - 1, halved=True)
            transposes(2, NG - 2)
            keep_clock(3)
            horner_1(NG - 1, halved=True)
            pair_products(NG - 2, hT_low_ok[1], NG)
            horner_0(NG - 1, halved=True)
            transposes_3(NG - 3)
            pair_self(NG - 2)
            keep_clock(2)
            learnt_h(NG - 3)
            keep_clock(4)
            pair_upper(NG - 2)
            keep_clock(1)
            transposes(2, NG - 1)
            keep_clock(7)
            pair_lower(NG - 2)
            learnt_out(NG - 3)
            pair_products(NG - 1, t_min_ok, NG - 1)
            keep_clock(4)
            pair_self(NG - 1)
            keep_clock(2)
            transposes_3(NG - 2)
            keep_clock(1)
            pair_upper(NG - 1)
            keep_clock(4)
            pair_lower(NG - 1)
            learnt_h(NG - 2)
            keep_clock(11)
            last_transposes_3()
            learnt_out(NG - 2)
            last_learnt()


_INS = ['x', 'adj', 'L0_gnn_q', 'L0_gnn_k', 'L0_gnn_v', 'L1_gnn_weight_1', 'L2_gnn_others_weight',
        'L2_gnn_self_weight', 'L2_gnn_att_weight', 'L3_gnn_W', 'L3_gnn_e', 'L3_gnn_bias']


def kernel(**inputs):
    import numpy as _np
    import concourse.bacc as _bacc
    from concourse import mybir as _mybir
    from concourse.bass_utils import run_bass_kernel_spmd as _run

    nc = _bacc.Bacc("TRN2", target_bir_lowering=False, num_devices=1)
    arrays, args = {}, []
    for name in _INS:
        a = _np.ascontiguousarray(inputs[name])
        arrays[f"in_{name}_dram"] = a
        args.append(nc.dram_tensor(f"in_{name}_dram", a.shape, _mybir.dt.from_np(a.dtype), kind="ExternalInput").ap())
    out = nc.dram_tensor("out_dram", inputs["x"].shape, _mybir.dt.float32, kind="ExternalOutput").ap()
    four_layer_gnn(nc, *args, out)
    r = _run(nc, [arrays], core_ids=[0])
    return r.results[0]["out_dram"]
```
